# Optimizing a Trainium2 kernel written in Bass

```python
import numpy as np
import jax
import jax.numpy as jnp

def _softmax(x, axis=-1):
    return jax.nn.softmax(x, axis=axis)
def _gelu(x):
    return jax.nn.gelu(x, approximate=True)
def _silu(x):
    return jax.nn.silu(x)
def _sigmoid(x):
    return jax.nn.sigmoid(x)
def _layernorm(x, axis=-1, eps=1e-5):
    m = jnp.mean(x, axis=axis, keepdims=True)
    v = jnp.var(x, axis=axis, keepdims=True)
    return (x - m) / jnp.sqrt(v + eps)
def _scatter_add(tgt, idx, src, axis=0):
    return tgt.at[idx].add(src)
def _segment_sum(src, seg, n):
    return jax.ops.segment_sum(src, seg, n)

kernel_name = 'mk_dlrm_tower_d1_rec_c0a25e'

def setup_inputs(seed: int = 0):
    np.random.seed(seed)
    _w = jnp.asarray
    def _rec_inputs():
        import jax
        import jax.numpy as jnp
        _tk = jax.random.key(seed)
        ids = jnp.stack([jax.random.randint(jax.random.fold_in(_tk, 200 + f), (1024,), 0, v, jnp.int32) for f, v in enumerate([1000000, 10000, 10000, 100000])], axis=1)
        tbl_0 = 0.05 * jax.random.normal(jax.random.fold_in(_tk, 500 + 0), (1000000, 4), jnp.float32)
        tbl_1 = 0.05 * jax.random.normal(jax.random.fold_in(_tk, 500 + 1), (10000, 4), jnp.float32)
        tbl_2 = 0.05 * jax.random.normal(jax.random.fold_in(_tk, 500 + 2), (10000, 4), jnp.float32)
        tbl_3 = 0.05 * jax.random.normal(jax.random.fold_in(_tk, 500 + 3), (100000, 4), jnp.float32)
        _rk = jax.random.fold_in(_tk, 7)
        r_x = 7.22013e-05 + 1.00017 * jax.random.normal(jax.random.fold_in(_rk, 101), (1024, 2048), jnp.float32)
        W_top1 = 0.0197642 * jax.random.normal(jax.random.fold_in(_tk, 801), (2560, 512), jnp.float32)
        W_top2 = 0.0441942 * jax.random.normal(jax.random.fold_in(_tk, 802), (512, 256), jnp.float32)
        W_top3 = 0.0625 * jax.random.normal(jax.random.fold_in(_tk, 803), (256, 1), jnp.float32)
        b_top1 = jnp.zeros((512,), jnp.float32)
        b_top2 = jnp.zeros((256,), jnp.float32)
        return r_x, ids, tbl_0, tbl_1, tbl_2, tbl_3, W_top1, b_top1, W_top2, b_top2, W_top3
    r_x, ids, tbl_0, tbl_1, tbl_2, tbl_3, W_top1, b_top1, W_top2, b_top2, W_top3 = _rec_inputs()
    def _L0_rec_setup():
        import jax, jax.numpy as jnp
        import numpy as np
        B, IN, HID, D, N, OUT = (4096, 2048, 2048, 512, 4, 512)
        H = 8
        HD = D // H

        def _ln(x, g, b):
            m = x.mean(-1, keepdims=True)
            v = ((x - m) ** 2).mean(-1, keepdims=True)
            return (x - m) / jnp.sqrt(v + 1e-05) * g + b
        key = jax.random.key(seed)
        ks = jax.random.split(key, 32)

        def nrm(k, shape, scale=0.02):
            return jax.random.normal(k, shape, jnp.float32) * scale
        inp = {}
        inp['x'] = jax.random.normal(ks[0], (B, IN), jnp.float32)
        inp['strength'] = jax.random.uniform(ks[1], (B, N, N), jnp.float32)
        for t, i in (('er', 2), ('ei', 4)):
            inp[t + '_W1'] = nrm(ks[i], (HID, IN))
            inp[t + '_b1'] = jnp.zeros((HID,), jnp.float32)
            inp[t + '_g1'] = jnp.ones((HID,), jnp.float32)
            inp[t + '_be1'] = jnp.zeros((HID,), jnp.float32)
            inp[t + '_W2'] = nrm(ks[i + 1], (N * D, HID))
            inp[t + '_b2'] = jnp.zeros((N * D,), jnp.float32)
        names = ['Wq_r', 'Wq_i', 'Wk_r', 'Wk_i', 'Wv_r', 'Wv_i', 'Wo_r', 'Wo_i']
        for j, nm in enumerate(names):
            inp[nm] = nrm(ks[6 + j], (D, D))
            inp['b' + nm[1:]] = jnp.zeros((D,), jnp.float32)
        inp['int_Wr'] = jnp.tile(jnp.eye(D, dtype=jnp.float32)[None], (N, 1, 1))
        inp['int_Wi'] = jnp.zeros((N, D, D), jnp.float32)
        inp['meas_Mr'] = nrm(ks[20], (OUT, D), 1.0 / np.sqrt(D))
        inp['meas_Mi'] = nrm(ks[21], (OUT, D), 1.0 / np.sqrt(D))
        inp['post_W'] = nrm(ks[22], (OUT, OUT))
        inp['post_b'] = jnp.zeros((OUT,), jnp.float32)
        inp['post_g'] = jnp.ones((OUT,), jnp.float32)
        inp['post_be'] = jnp.zeros((OUT,), jnp.float32)
        return inp
    _L0_rec_all = _L0_rec_setup()
    _L0_rec_in = {k: v for k, v in _L0_rec_all.items() if k in ('er_W1', 'er_b1', 'er_g1', 'er_be1', 'er_W2', 'er_b2', 'ei_W1', 'ei_b1', 'ei_g1', 'ei_be1', 'ei_W2', 'ei_b2', 'Wq_r', 'bq_r', 'Wq_i', 'bq_i', 'Wk_r', 'bk_r', 'Wk_i', 'bk_i', 'Wv_r', 'bv_r', 'Wv_i', 'bv_i', 'Wo_r', 'bo_r', 'Wo_i', 'bo_i', 'int_Wr', 'int_Wi', 'meas_Mr', 'meas_Mi', 'post_W', 'post_b', 'post_g', 'post_be', )}
    del _L0_rec_all

    return {
        "r_x": r_x,
        "ids": ids,
        "tbl_0": tbl_0,
        "tbl_1": tbl_1,
        "tbl_2": tbl_2,
        "tbl_3": tbl_3,
        "W_top1": W_top1,
        "b_top1": b_top1,
        "W_top2": W_top2,
        "b_top2": b_top2,
        "W_top3": W_top3,
        "L0_rec_er_W1": _L0_rec_in["er_W1"],
        "L0_rec_er_b1": _L0_rec_in["er_b1"],
        "L0_rec_er_g1": _L0_rec_in["er_g1"],
        "L0_rec_er_be1": _L0_rec_in["er_be1"],
        "L0_rec_er_W2": _L0_rec_in["er_W2"],
        "L0_rec_er_b2": _L0_rec_in["er_b2"],
        "L0_rec_ei_W1": _L0_rec_in["ei_W1"],
        "L0_rec_ei_b1": _L0_rec_in["ei_b1"],
        "L0_rec_ei_g1": _L0_rec_in["ei_g1"],
        "L0_rec_ei_be1": _L0_rec_in["ei_be1"],
        "L0_rec_ei_W2": _L0_rec_in["ei_W2"],
        "L0_rec_ei_b2": _L0_rec_in["ei_b2"],
        "L0_rec_Wq_r": _L0_rec_in["Wq_r"],
        "L0_rec_bq_r": _L0_rec_in["bq_r"],
        "L0_rec_Wq_i": _L0_rec_in["Wq_i"],
        "L0_rec_bq_i": _L0_rec_in["bq_i"],
        "L0_rec_Wk_r": _L0_rec_in["Wk_r"],
        "L0_rec_bk_r": _L0_rec_in["bk_r"],
        "L0_rec_Wk_i": _L0_rec_in["Wk_i"],
        "L0_rec_bk_i": _L0_rec_in["bk_i"],
        "L0_rec_Wv_r": _L0_rec_in["Wv_r"],
        "L0_rec_bv_r": _L0_rec_in["bv_r"],
        "L0_rec_Wv_i": _L0_rec_in["Wv_i"],
        "L0_rec_bv_i": _L0_rec_in["bv_i"],
        "L0_rec_Wo_r": _L0_rec_in["Wo_r"],
        "L0_rec_bo_r": _L0_rec_in["bo_r"],
        "L0_rec_Wo_i": _L0_rec_in["Wo_i"],
        "L0_rec_bo_i": _L0_rec_in["bo_i"],
        "L0_rec_int_Wr": _L0_rec_in["int_Wr"],
        "L0_rec_int_Wi": _L0_rec_in["int_Wi"],
        "L0_rec_meas_Mr": _L0_rec_in["meas_Mr"],
        "L0_rec_meas_Mi": _L0_rec_in["meas_Mi"],
        "L0_rec_post_W": _L0_rec_in["post_W"],
        "L0_rec_post_b": _L0_rec_in["post_b"],
        "L0_rec_post_g": _L0_rec_in["post_g"],
        "L0_rec_post_be": _L0_rec_in["post_be"],
    }

def reference(r_x, ids, tbl_0, tbl_1, tbl_2, tbl_3, W_top1, b_top1, W_top2, b_top2, W_top3, L0_rec_er_W1, L0_rec_er_b1, L0_rec_er_g1, L0_rec_er_be1, L0_rec_er_W2, L0_rec_er_b2, L0_rec_ei_W1, L0_rec_ei_b1, L0_rec_ei_g1, L0_rec_ei_be1, L0_rec_ei_W2, L0_rec_ei_b2, L0_rec_Wq_r, L0_rec_bq_r, L0_rec_Wq_i, L0_rec_bq_i, L0_rec_Wk_r, L0_rec_bk_r, L0_rec_Wk_i, L0_rec_bk_i, L0_rec_Wv_r, L0_rec_bv_r, L0_rec_Wv_i, L0_rec_bv_i, L0_rec_Wo_r, L0_rec_bo_r, L0_rec_Wo_i, L0_rec_bo_i, L0_rec_int_Wr, L0_rec_int_Wi, L0_rec_meas_Mr, L0_rec_meas_Mi, L0_rec_post_W, L0_rec_post_b, L0_rec_post_g, L0_rec_post_be):
    import jax
    import jax.numpy as jnp
    def _L0_rec_ref(x, strength, er_W1, er_b1, er_g1, er_be1, er_W2, er_b2, ei_W1, ei_b1, ei_g1, ei_be1, ei_W2, ei_b2, Wq_r, bq_r, Wq_i, bq_i, Wk_r, bk_r, Wk_i, bk_i, Wv_r, bv_r, Wv_i, bv_i, Wo_r, bo_r, Wo_i, bo_i, int_Wr, int_Wi, meas_Mr, meas_Mi, post_W, post_b, post_g, post_be):
        import jax, jax.numpy as jnp
        import numpy as np
        B, IN, HID, D, N, OUT = (4096, 2048, 2048, 512, 4, 512)
        H = 8
        HD = D // H

        def _ln(x, g, b):
            m = x.mean(-1, keepdims=True)
            v = ((x - m) ** 2).mean(-1, keepdims=True)
            return (x - m) / jnp.sqrt(v + 1e-05) * g + b
        Bsz = x.shape[0]

        def enc(W1, b1, g, be, W2, b2):
            h = jax.nn.gelu(_ln(x @ W1.T + b1, g, be), approximate=False)
            return (h @ W2.T + b2).reshape(Bsz, N, D)
        sr = enc(er_W1, er_b1, er_g1, er_be1, er_W2, er_b2)
        si = enc(ei_W1, ei_b1, ei_g1, ei_be1, ei_W2, ei_b2)

        def heads(t):
            return t.reshape(Bsz, N, H, HD).transpose(0, 2, 1, 3)
        qr = heads(sr @ Wq_r.T + bq_r)
        qi = heads(si @ Wq_i.T + bq_i)
        kr = heads(sr @ Wk_r.T + bk_r)
        ki = heads(si @ Wk_i.T + bk_i)
        vr = heads(sr @ Wv_r.T + bv_r)
        vi = heads(si @ Wv_i.T + bv_i)
        ar = jnp.einsum('bhnd,bhmd->bhnm', qr, kr) + jnp.einsum('bhnd,bhmd->bhnm', qi, ki)
        ai = jnp.einsum('bhnd,bhmd->bhnm', qi, kr) - jnp.einsum('bhnd,bhmd->bhnm', qr, ki)
        mag = jnp.sqrt(ar ** 2 + ai ** 2 + 1e-08) * HD ** (-0.5)
        w = jax.nn.softmax(mag, axis=-1)
        out_r = jnp.einsum('bhnm,bhmd->bhnd', w, vr).transpose(0, 2, 1, 3).reshape(Bsz, N, D)
        out_i = jnp.einsum('bhnm,bhmd->bhnd', w, vi).transpose(0, 2, 1, 3).reshape(Bsz, N, D)
        attn_r = out_r @ Wo_r.T + bo_r
        attn_i = out_i @ Wo_i.T + bo_i
        R = jnp.einsum('bnd,ned->bne', attn_r, int_Wr) - jnp.einsum('bnd,ned->bne', attn_i, int_Wi)
        I = jnp.einsum('bnd,ned->bne', attn_r, int_Wi) + jnp.einsum('bnd,ned->bne', attn_i, int_Wr)
        Ri, Ii = (R[:, :, None, :], I[:, :, None, :])
        Rj, Ij = (R[:, None, :, :], I[:, None, :, :])
        phase = jnp.arctan2(Ii * Rj - Ri * Ij, Ri * Rj + Ii * Ij)
        f = jnp.cos(phase) * strength[..., None]
        sup_r = jnp.einsum('bijd,bjd->bd', f, R)
        sup_i = jnp.einsum('bijd,bjd->bd', f, I)
        norm = jnp.sqrt(jnp.sum(sup_r ** 2 + sup_i ** 2, axis=-1, keepdims=True) + 1e-08)
        sup_r = sup_r / norm
        sup_i = sup_i / norm
        mr = sup_r @ meas_Mr.T - sup_i @ meas_Mi.T
        mi = sup_r @ meas_Mi.T + sup_i @ meas_Mr.T
        amp = jnp.sqrt(mr ** 2 + mi ** 2)
        out = jax.nn.gelu(_ln(amp @ post_W.T + post_b, post_g, post_be), approximate=False)
        return out

    e = jnp.stack([tbl_0[ids[:, 0]], tbl_1[ids[:, 1]], tbl_2[ids[:, 2]], tbl_3[ids[:, 3]]], axis=1)
    z = _L0_rec_ref(r_x, e, L0_rec_er_W1, L0_rec_er_b1, L0_rec_er_g1, L0_rec_er_be1, L0_rec_er_W2, L0_rec_er_b2, L0_rec_ei_W1, L0_rec_ei_b1, L0_rec_ei_g1, L0_rec_ei_be1, L0_rec_ei_W2, L0_rec_ei_b2, L0_rec_Wq_r, L0_rec_bq_r, L0_rec_Wq_i, L0_rec_bq_i, L0_rec_Wk_r, L0_rec_bk_r, L0_rec_Wk_i, L0_rec_bk_i, L0_rec_Wv_r, L0_rec_bv_r, L0_rec_Wv_i, L0_rec_bv_i, L0_rec_Wo_r, L0_rec_bo_r, L0_rec_Wo_i, L0_rec_bo_i, L0_rec_int_Wr, L0_rec_int_Wi, L0_rec_meas_Mr, L0_rec_meas_Mi, L0_rec_post_W, L0_rec_post_b, L0_rec_post_g, L0_rec_post_be)
    z = z.reshape(z.shape[0], -1)
    h = jnp.concatenate([z, r_x], axis=1)
    h = jnp.maximum(h @ W_top1 + b_top1, 0.0)
    h = jnp.maximum(h @ W_top2 + b_top2, 0.0)
    y = h @ W_top3
    return y


_drawn_inputs = setup_inputs


def setup_inputs(seed=0):
    import zlib

    import numpy as np

    out = dict(_drawn_inputs(seed))
    spreads = {'b_top1': (0.0, 0.1),
     'b_top2': (0.0, 0.1),
     'L0_rec_er_b1': (0.0, 0.8),
     'L0_rec_er_g1': (1.0, 0.6),
     'L0_rec_er_be1': (0.0, 0.8),
     'L0_rec_er_b2': (0.0, 0.8),
     'L0_rec_ei_b1': (0.0, 0.8),
     'L0_rec_ei_g1': (1.0, 0.6),
     'L0_rec_ei_be1': (0.0, 0.8),
     'L0_rec_ei_b2': (0.0, 0.8),
     'L0_rec_bq_r': (0.0, 0.8),
     'L0_rec_bq_i': (0.0, 0.8),
     'L0_rec_bk_r': (0.0, 0.8),
     'L0_rec_bk_i': (0.0, 0.8),
     'L0_rec_bv_r': (0.0, 0.1),
     'L0_rec_bv_i': (0.0, 0.1),
     'L0_rec_bo_r': (0.0, 0.1),
     'L0_rec_bo_i': (0.0, 0.1),
     'L0_rec_int_Wi': (0.0, 0.1),
     'L0_rec_post_b': (0.0, 0.1),
     'L0_rec_post_g': (1.0, 0.2),
     'L0_rec_post_be': (0.0, 0.1)}
    factors = {'L0_rec_Wq_r': 8.0, 'L0_rec_Wq_i': 8.0, 'L0_rec_Wk_r': 8.0, 'L0_rec_Wk_i': 8.0}
    for name, (base, spread) in spreads.items():
        noise = np.random.default_rng([zlib.crc32(name.encode()), seed]).standard_normal(out[name].shape)
        drawn = base * np.exp(spread * noise) if base else spread * noise
        out[name] = jnp.asarray(drawn.astype(out[name].dtype))
    for name, factor in factors.items():
        out[name] = (out[name] * factor).astype(out[name].dtype)
    return out
```

```python
from contextlib import ExitStack

import concourse.bass as bass
import concourse.mybir as mybir

F32 = mybir.dt.float32
F32R = mybir.dt.float32r
BF16 = mybir.dt.bfloat16
U32 = mybir.dt.uint32
ACT = mybir.ActivationFunctionType
ALU = mybir.AluOpType
AX = mybir.AxisListType

P = 128
TOK = 1024
IN, HID, D, N, OUT = 2048, 2048, 512, 4, 512
H = 8
HD = D // H
TOP1, TOP2 = 512, 256
LN_EPS = 1e-5
TINY = 1e-8
W = 512

TT = TOK // P
BT = 64
GB = P // N
KI = IN // P
KD = D // P
CHUNKS_A = 2 * HID // W + 1
MT = N * D // P
RAW = 4
SPL = 4

COL_B2 = 4 * KI
COL_BC = 4 * KI + 2 * MT
COL_PG = COL_BC + 8 * KD
COL_PBE = COL_PG + KD
NCOL = COL_PBE + KD
PC_ATT, PC_INT, PC_TOP = 0, 8 * KD, 8 * KD + 2 * N * KD
N_TOP = 2 * KD + KD + KD + KD // 2
NPIECE = PC_TOP + N_TOP


def split3(mm, out, ahi, alo, bhi, blo, first, last):
    mm(out, ahi, bhi, start=first, stop=False)
    mm(out, ahi, blo, start=False, stop=False)
    return mm(out, alo, bhi, start=False, stop=last)


class Stage:

    def __init__(self, nc, tag):
        self.nc, self.tag, self.ctx = nc, tag, ExitStack()

    def sb(self, name, shape, dt=F32):
        return self.ctx.enter_context(self.nc.sbuf_tensor(f"{self.tag}_{name}", shape, dt))

    def sem(self, name):
        return self.ctx.enter_context(self.nc.semaphore(f"{self.tag}_{name}"))


def phase_constants(nc, g):
    s = Stage(nc, "c")
    with s.ctx:
        zeroed = s.sem("zeroed")
        made = s.sem("made")
        cols_in = s.sem("cols_in")
        block = s.ctx.enter_context(nc.Block())

        @block.sync
        def _(sp):
            sp.dma_start(g.cols[:, :], g.cols_in).then_inc(cols_in, 16)
            sp.wait_ge(cols_in, 16)

        @block.gpsimd
        def _(pool):
            pool.memset(g.ident[:, :], 0.0).then_inc(zeroed, 1)
            pool.memset(g.mask[:, :, :], 0.0).then_inc(zeroed, 1)
            pool.memset(g.eps_ln[:, :], LN_EPS).then_inc(zeroed, 1)
            pool.memset(g.tiny[:, :], TINY).then_inc(zeroed, 1)
            pool.memset(g.tiny_hd[:, :], TINY / HD).then_inc(zeroed, 1)
            pool.memset(g.none[:, :], 0.0).then_inc(zeroed, 1)
            pool.wait_ge(zeroed, 6)
            pool.affine_select(out=g.ident[:, :], in_=g.ident[:, :], compare_op=ALU.not_equal, fill=1.0, base=0,
                               pattern=[[-1, P]], channel_multiplier=1).then_inc(made, 1)
            for q in range(N):
                pool.wait_ge(made, q + 1)
                pool.affine_select(out=g.mask[:, :, :], in_=g.mask[:, :, :], compare_op=ALU.not_equal, fill=1.0,
                                   base=-GB * q, pattern=[[0, N], [-1, GB]], channel_multiplier=1).then_inc(made, 1)
            pool.wait_ge(made, N + 1)


def phase_first_layers(nc, g):
    s = Stage(nc, "a")
    XRAW = 4
    with s.ctx:
        xraw = s.sb("xraw", [P, XRAW, TOK])
        xhi = s.sb("xhi", [P, KI, TOK], F32R)
        xlo = s.sb("xlo", [P, KI, TOK], F32R)
        wraw = s.sb("wraw", [P, RAW, W])
        whi = s.sb("whi", [P, SPL, W], F32R)
        wlo = s.sb("wlo", [P, SPL, W], F32R)
        bias = s.sb("bias", [P, CHUNKS_A * W])
        hst = s.sb("hst", [P, TT, W])
        x_loaded = [s.sem(f"x_loaded{i}") for i in range(XRAW)]
        x_hi = s.sem("x_hi")
        x_split = s.sem("x_split")
        w_loaded = [s.sem(f"w_loaded{i}") for i in range(RAW)]
        w_hi = s.sem("w_hi")
        w_split = s.sem("w_split")
        w_used = s.sem("w_used")
        bank_full = s.sem("bank_full")
        bank_read = s.sem("bank_read")
        stats_done = s.sem("stats_done")
        bias_in = s.sem("bias_in")
        stored = [s.sem(f"stored{i}") for i in range(TT)]
        block = s.ctx.enter_context(nc.Block())

        @block.sync
        def _(sp):
            sp.dma_start(bias[:, :], g.row1.rearrange("c n -> (c n)").partition_broadcast(P)).then_inc(bias_in, 16)
            with sp.Fori(0, CHUNKS_A) as c:
                for k in range(KI):
                    sp.wait_ge(w_split, c * KI + (k + 1))
                    sp.dma_start(wraw[:, k % RAW, :], g.w_first[c, k]).then_inc(w_loaded[k % RAW], 16)

        @block.gpsimd
        def _(pool):
            for k in range(KI):
                if k >= XRAW:
                    pool.wait_ge(x_split, k - XRAW + 1)
                pool.dma_start(xraw[:, k % XRAW, :], g.x_t[k]).then_inc(x_loaded[k % XRAW], 16)
            with pool.Fori(0, CHUNKS_A) as c:
                for t in range(TT):
                    pool.wait_ge(bank_read, c * TT + (TT + t + 1))
                    pool.dma_start(g.h_scr[c, t], hst[:, t, :]).then_inc(stored[t], 16)
            for t in range(TT):
                pool.wait_ge(stored[t], 16 * CHUNKS_A)
            pool.wait_ge(stats_done, TT * CHUNKS_A)

        @block.scalar
        def _(act):
            def w_high(c, k):
                act.wait_ge(w_loaded[k % RAW], c * (16 * KI // RAW) + 16 * (k // RAW + 1))
                act.wait_ge(w_used, c * KI + (k + 1))
                act.activation(whi[:, k % SPL, :], wraw[:, k % RAW, :], ACT.Copy).then_inc(w_hi, 1)

            for k in range(KI):
                act.wait_ge(x_loaded[k % XRAW], 16 * (k // XRAW + 1))
                act.activation(xhi[:, k, :], xraw[:, k % XRAW, :], ACT.Copy).then_inc(x_hi, 1)
                w_high(0, k)
            with act.Fori(1, CHUNKS_A) as c:
                for k in range(KI):
                    w_high(c, k)

        @block.vector
        def _(dve):
            def w_low(c, k):
                dve.wait_ge(w_hi, c * KI + (k + 1))
                dve.tensor_tensor(wlo[:, k % SPL, :], wraw[:, k % RAW, :], whi[:, k % SPL, :].bitcast(F32),
                                  ALU.subtract).then_inc(w_split, 1)

            def evacuate(c):
                for t in range(TT):
                    dve.wait_ge(bank_full, c * TT + (t + 1))
                    dve.wait_ge(stored[t], c * 16)
                    dve.wait_ge(stats_done, c * TT)
                    dve.tensor_tensor(hst[:, t, :], g.ps[:, t, :], bias[:, bass.ts(c, W)],
                                      ALU.add).then_inc(bank_read, 1)
                for t in range(TT):
                    dve.wait_ge(bank_read, c * TT + (TT + t + 1))
                    dve.bn_stats(g.stats[:, bass.ds(c * TT + t, 1), :], hst[:, t, :]).then_inc(stats_done, 1)

            dve.sem_inc(w_split, RAW)
            for k in range(KI):
                dve.wait_ge(x_hi, k + 1)
                dve.tensor_tensor(xlo[:, k, :], xraw[:, k % XRAW, :], xhi[:, k, :].bitcast(F32),
                                  ALU.subtract).then_inc(x_split, 1)
                w_low(0, k)
            dve.wait_ge(bias_in, 16)
            AHEAD = 3
            for k in range(AHEAD):
                w_low(1, k)
            evacuate(0)
            with dve.Fori(1, CHUNKS_A - 1) as c:
                for k in range(AHEAD, KI):
                    w_low(c, k)
                for k in range(AHEAD):
                    w_low(c + 1, k)
                evacuate(c)
            for k in range(AHEAD, KI):
                w_low(CHUNKS_A - 1, k)
            evacuate(CHUNKS_A - 1)

        @block.tensor
        def _(pe):
            pe.sem_inc(w_used, SPL)
            pe.sem_inc(bank_read, TT)
            with pe.Fori(0, CHUNKS_A) as c:
                for k in range(KI):
                    pe.wait_ge(x_split, k + 1)
                    pe.wait_ge(w_split, c * KI + (RAW + k + 1))
                    for t in range(TT):
                        if k == 0:
                            pe.wait_ge(bank_read, c * TT + (t + 1))
                        m = split3(pe.matmul, g.ps[:, t, :], xhi[:, k, t * P:(t + 1) * P], xlo[:, k, t * P:(t + 1) * P],
                                   whi[:, k % SPL, :], wlo[:, k % SPL, :], k == 0, k == KI - 1)
                        if k == KI - 1 and t < TT - 1:
                            m.then_inc(bank_full, 1)
                    if k < KI - 1:
                        m.then_inc(w_used, 1)
                m.then_inc(bank_full, 1)
                pe.drain().then_inc(w_used, 1)


def phase_second_layers(nc, g):
    s = Stage(nc, "b")
    CH, ST = 8, 8
    HW = 256
    AHEAD = 3
    with s.ctx:
        ghi = s.sb("ghi", [P, KI, TOK], F32R)
        glo = s.sb("glo", [P, KI, TOK], F32R)
        wraw = s.sb("wraw", [P, RAW, W])
        whi = s.sb("whi", [P, SPL, 2, 256], F32R)
        wlo = s.sb("wlo", [P, SPL, 2, 256], F32R)
        hl = s.sb("hl", [P, 2, TT, HW])
        gf = s.sb("gf", [P, 2, TOK])
        shi = s.sb("shi", [P, 2, W // GB, 2, GB], F32R)
        slo = s.sb("slo", [P, 2, W // GB, 2, GB], F32R)
        mv = s.sb("mv", [P, 2 * TT, 2])
        rstd = s.sb("rstd", [P, 2 * TT])
        b2 = s.sb("b2", [P, 2])
        b2_ready = s.sem("b2_ready")
        mv_done = s.sem("mv_done")
        std_done = s.sem("std_done")
        rstd_done = s.sem("rstd_done")
        w_loaded = [s.sem(f"w_loaded{i}") for i in range(RAW)]
        w_hi = s.sem("w_hi")
        w_split = s.sem("w_split")
        w_used = s.sem("w_used")
        h_loaded = [s.sem(f"h_loaded{i}") for i in range(2)]
        h_normed = s.sem("h_normed")
        turned = s.sem("turned")
        gelu_done = s.sem("gelu_done")
        g_hi = s.sem("g_hi")
        g_split = s.sem("g_split")
        acc_full = s.sem("acc_full")
        s_hi = s.sem("s_hi")
        s_split = s.sem("s_split")
        st_hi = [s.sem(f"stored_hi{i}") for i in range(2)]
        st_lo = [s.sem(f"stored_lo{i}") for i in range(2)]
        block = s.ctx.enter_context(nc.Block())
        acc = [g.ps[:, 4 + i, :] for i in range(4)]

        @block.sync
        def _(sp):
            with sp.Fori(0, 2 * CH) as c:
                for j in range(ST):
                    sp.wait_ge(w_split, c * ST + (j + 1))
                    sp.dma_start(wraw[:, j % RAW, :], g.w_second[c, j]).then_inc(w_loaded[j % RAW], 16)

        @block.gpsimd
        def _(pool):
            def load_h(br, j):
                pool.wait_ge(turned, br * KI + (2 * j + 2))
                src = g.h_scr[br * 4 + j // 2, :, :, (j % 2) * HW:(j % 2) * HW + HW]
                pool.dma_start(hl[:, j % 2, :, :], src.rearrange("t p f -> p t f")).then_inc(h_loaded[j % 2], 16)

            load_h(0, 0)
            load_h(0, 1)
            for br in range(2):
                for j in range(2, ST):
                    load_h(br, j)
                if br == 0:
                    load_h(1, 0)
                    load_h(1, 1)
                with pool.Fori(0, KD) as k:
                    for pair in range(2):
                        for half in range(2):
                            for h, t, done, sent in ((0, shi, s_hi, st_hi), (1, slo, s_split, st_lo)):
                                pool.wait_ge(done, br * (4 * CH) + k * 8 + (4 * pair + 2 * half + 2 + 4 * h))
                                dst = g.s_scr.rearrange(
                                        "e h c p k n b -> p e h c k (n b)")[
                                    :, br:br + 1, h, half * (W // GB):(half + 1) * (W // GB), bass.ds(k, 1),
                                    2 * pair * GB:2 * pair * GB + 2 * GB]
                                pool.dma_start(dst.rearrange("p e c k x -> p (e c k) x"),
                                               t[:, half, :, :, :].bitcast(F32).rearrange("p c n b -> p c (n b)")).then_inc(
                                                   sent[half], 16)
            for half in range(2):
                pool.wait_ge(st_hi[half], 16 * 2 * CH)
                pool.wait_ge(st_lo[half], 16 * 2 * CH)

        @block.scalar
        def _(act):
            def w_high(c, j):
                act.wait_ge(w_loaded[j % RAW], c * (16 * ST // RAW) + 16 * (j // RAW + 1))
                act.wait_ge(w_used, c * ST + (j + 1))
                act.activation(whi[:, j % SPL, :, :].rearrange("p a n -> p (a n)"), wraw[:, j % RAW, :],
                               ACT.Copy).then_inc(w_hi, 1)

            def s_high(br, c):
                for b in range(4):
                    cc = br * CH + c
                    act.wait_ge(acc_full, cc * 4 + (b + 1))
                    act.wait_ge(st_hi[b // 2], cc * 16)
                    act.wait_ge(b2_ready, cc + 1)
                    act.activation(shi[:, b // 2, :, b % 2, :], acc[b].rearrange("p (g b) -> p g b", b=GB), ACT.Identity,
                                   bias=b2[:, b % 2:b % 2 + 1]).then_inc(s_hi, 1)

            def gain_shift(br, x, k):
                i = (2 * br + x) * KI + k
                return g.cols[:, i:i + 1]

            act.wait_ge(mv_done, 2 * TT)
            act.activation(rstd[:, :], mv[:, :, 1], ACT.Sqrt, bias=g.eps_ln[:, :]).then_inc(std_done, 1)
            for br in range(2):
                for j in range(ST):
                    w_high(br * CH, j)
                    for k in (2 * j, 2 * j + 1):
                        act.wait_ge(turned, br * KI + (4 + k + 1))
                        act.wait_ge(g_split, br * KI + (k + 1))
                        if k == 0:
                            act.wait_ge(w_used, br * (CH * ST) + SPL)
                        act.activation(gf[:, k % 2, :], g.ps[:, 2 * (k % 2):2 * (k % 2) + 2, :].rearrange("p a n -> p (a n)"),
                                       ACT.Gelu, bias=gain_shift(br, 1, k),
                                       scale=gain_shift(br, 0, k)).then_inc(gelu_done, 1)
                        act.wait_ge(gelu_done, br * KI + (2 + k + 1))
                        act.activation(ghi[:, k, :], gf[:, k % 2, :], ACT.Copy).then_inc(g_hi, 1)
                for j in range(AHEAD):
                    w_high(br * CH + 1, j)
                s_high(br, 0)
                with act.Fori(1, CH - 1) as c:
                    for j in range(AHEAD, ST):
                        w_high(br * CH + c, j)
                    for j in range(AHEAD):
                        w_high(br * CH + c + 1, j)
                    s_high(br, c)
                for j in range(AHEAD, ST):
                    w_high(br * CH + (CH - 1), j)
                s_high(br, CH - 1)

        @block.vector
        def _(dve):
            def w_low(c, j):
                dve.wait_ge(w_hi, c * ST + (j + 1))
                dve.tensor_tensor(wlo[:, j % SPL, :, :].rearrange("p a n -> p (a n)"), wraw[:, j % RAW, :],
                                  whi[:, j % SPL, :, :].bitcast(F32).rearrange("p a n -> p (a n)"),
                                  ALU.subtract).then_inc(w_split, 1)

            def chunk_bias(cc):
                dve.tensor_copy(b2[:, :], g.cols[:, bass.ds(cc * 2 + COL_B2, 2)]).then_inc(b2_ready, 1)

            def s_low(br, c):
                chunk_bias(br * CH + c)
                dve.wait_ge(b2_ready, br * CH + (c + 1))
                for b in range(4):
                    cc = br * CH + c
                    dve.wait_ge(s_hi, cc * 4 + (b + 1))
                    dve.wait_ge(st_lo[b // 2], cc * 16)
                    dve.scalar_tensor_tensor(out=slo[:, b // 2, :, b % 2, :],
                                             in0=acc[b].rearrange("p (g b) -> p g b", b=GB),
                                             scalar=b2[:, b % 2:b % 2 + 1],
                                             in1=shi[:, b // 2, :, b % 2, :].bitcast(F32), op0=ALU.add,
                                             op1=ALU.subtract).then_inc(s_split, 1)

            def normalise(br, j):
                dve.wait_ge(h_loaded[j % 2], br * (16 * ST // 2) + 16 * (j // 2 + 1))
                for t in range(TT):
                    i = br * TT + t
                    m = dve.tensor_scalar(hl[:, j % 2, t, :], hl[:, j % 2, t, :], mv[:, i, 0:1], rstd[:, i:i + 1],
                                          ALU.subtract, ALU.mult)
                m.then_inc(h_normed, 1)

            dve.sem_inc(w_split, RAW)
            dve.sem_inc(g_split, 2)
            dve.sem_inc(s_split, 4)
            for br in range(2):
                for t in range(TT):
                    v = g.stats[:, :, :].rearrange("p (c t) s -> p c t s", t=TT)[:, 4 * br:4 * br + 4, t, :]
                    dve.bn_aggr(mv[:, br * TT + t, :], v).then_inc(mv_done, 1)
            dve.wait_ge(std_done, 1)
            dve.reciprocal(rstd[:, :], rstd[:, :]).then_inc(rstd_done, 1)
            dve.wait_ge(rstd_done, 1)
            for br in range(2):
                if br == 0:
                    normalise(0, 0)
                for j in range(ST):
                    w_low(br * CH, j)
                    if j + 1 < ST:
                        normalise(br, j + 1)
                    for k in (2 * j, 2 * j + 1):
                        dve.wait_ge(g_hi, br * KI + (k + 1))
                        dve.tensor_tensor(glo[:, k, :], gf[:, k % 2, :], ghi[:, k, :].bitcast(F32),
                                          ALU.subtract).then_inc(g_split, 1)
                for j in range(AHEAD):
                    w_low(br * CH + 1, j)
                s_low(br, 0)
                with dve.Fori(1, CH - 1) as c:
                    for j in range(AHEAD, ST):
                        w_low(br * CH + c, j)
                    for j in range(AHEAD):
                        w_low(br * CH + c + 1, j)
                    s_low(br, c)
                if br == 0:
                    normalise(1, 0)
                for j in range(AHEAD, ST):
                    w_low(br * CH + (CH - 1), j)
                s_low(br, CH - 1)

        @block.tensor
        def _(pe):
            def turn(br, k):
                pe.wait_ge(h_normed, br * ST + (k // 2 + 1))
                pe.wait_ge(gelu_done, br * KI + (k + 1))
                for t in range(TT):
                    m = pe.transpose(g.ps[:, 2 * (k % 2) + t // 4, (t % 4) * P:(t % 4 + 1) * P],
                                     hl[:, (k // 2) % 2, t, (k % 2) * P:(k % 2 + 1) * P], g.ident[:, :])
                m.then_inc(turned, 1)

            def multiply(cc, j, br=None):
                pe.wait_ge(w_split, cc * ST + (RAW + j + 1))
                if br is not None:
                    pe.wait_ge(g_split, br * KI + (2 + 2 * j + 2))
                for b in range(4):
                    half, m = b // 2, b % 2
                    if j == 0:
                        pe.wait_ge(s_split, cc * 4 + (b + 1))
                    for i in range(2):
                        k = 2 * j + i
                        cols = slice(half * W, half * W + W)
                        mm = split3(pe.matmul, acc[b], whi[:, j % SPL, i, m * P:(m + 1) * P],
                                    wlo[:, j % SPL, i, m * P:(m + 1) * P], ghi[:, k, cols], glo[:, k, cols],
                                    k == 0, k == KI - 1)
                    if j == ST - 1:
                        mm.then_inc(acc_full, 1)
                if j == ST - 1:
                    pe.drain().then_inc(w_used, 1)
                else:
                    mm.then_inc(w_used, 1)

            pe.sem_inc(w_used, SPL)
            pe.sem_inc(turned, 4)
            pe.sem_inc(gelu_done, 2)
            for br in range(2):
                if br == 0:
                    turn(0, 0)
                    turn(0, 1)
                for j in range(ST):
                    if j + 1 < ST:
                        turn(br, 2 * j + 2)
                        turn(br, 2 * j + 3)
                    multiply(br * CH, j, br)
                with pe.Fori(1, CH - 1) as c:
                    for j in range(ST):
                        multiply(br * CH + c, j)
                if br == 0:
                    turn(1, 0)
                    turn(1, 1)
                for j in range(ST):
                    multiply(br * CH + CH - 1, j)


def phase_attention(nc, g):
    s = Stage(nc, "t")
    NB = TOK // BT
    C = N * BT
    NG = BT // GB
    GH = NG * 2
    NP = 8 * KD
    TR = 2
    M_Q, M_K, M_V, M_O = 0, 2, 4, 6
    with s.ctx:
        wraw = s.sb("wraw", [P, TR, W])
        whi = s.sb("whi", [P, NP, W], F32R)
        wlo = s.sb("wlo", [P, NP, W], F32R)
        sx = s.sb("sx", [P, 2, 2, NG, KD, P], F32R)
        qk = s.sb("qk", [P, 2, 5, C])
        v = s.sb("v", [P, NG, 2, W])
        sq = s.sb("sq", [P, 2, W])
        m2 = s.sb("m2", [P, W])
        pd = s.sb("pd", [P, GH, N, GB])
        ptl = s.sb("ptl", [P, 2, W])
        sc = s.sb("sc", [P, 7, GH, N])
        ohi = s.sb("ohi", [P, KD, 2, C], F32R)
        olo = s.sb("olo", [P, KD, 2, C], F32R)
        ahi = s.sb("ahi", [P, 2, 2, C], F32R)
        alo = s.sb("alo", [P, 2, 2, C], F32R)
        w_loaded = [s.sem(f"w_loaded{i}") for i in range(TR)]
        w_hi = s.sem("w_hi")
        w_split = s.sem("w_split")
        s_loaded = s.sem("s_loaded")
        projected = s.sem("projected")
        q_read = s.sem("q_read")
        k_read = s.sem("k_read")
        v_full = s.sem("v_full")
        v_read = s.sem("v_read")
        scored = s.sem("scored")
        squared = s.sem("squared")
        step = s.sem("step")
        mag_done = s.sem("mag_done")
        exp_done = s.sem("exp_done")
        p_turned = s.sem("p_turned")
        pt_read = s.sem("pt_read")
        mixed = s.sem("mixed")
        o_hi = s.sem("o_hi")
        o_split = s.sem("o_split")
        wo_full = s.sem("wo_full")
        a_hi = s.sem("a_hi")
        a_split = s.sem("a_split")
        stored = [s.sem(f"stored{i}") for i in range(2)]
        block = s.ctx.enter_context(nc.Block())
        b_qk, b_sc, b_pt, b_mx = (g.ps[:, 2 * i:2 * i + 2, :] for i in range(4))
        RE, MAX = 0, 2

        def bcol(mat, m):
            return g.cols[:, COL_BC + mat * KD + m:COL_BC + mat * KD + m + 1]

        def by_group(ap):
            return ap.rearrange("p (g n b) -> p g n b", g=NG, n=N)

        def by_state(ap):
            return ap.rearrange("p (n g b) -> p g n b", g=NG, n=N)

        def blocks(eng, body):
            body(0, True, False)
            with eng.Fori(1, NB - 1) as b:
                body(b, False, False)
            body(NB - 1, False, True)

        @block.sync
        def _(sp):
            def load_s(b):
                for e in range(2):
                    for h in range(2):
                        src = g.s_scr[e, h].rearrange("c p k n b -> p c (k n b)")[:, bass.ds(b * NG, NG), :]
                        sp.dma_start(sx[:, e, h, :, :, :].bitcast(F32).rearrange("p g k c -> p g (k c)"),
                                     src).then_inc(s_loaded, 16)

            def store(b):
                for m in range(KD):
                    sp.wait_ge(a_split, b * 8 + (2 * m + 2))
                    for e in range(2):
                        for h, t in enumerate((ahi, alo)):
                            dst = g.a_scr.rearrange("b n p v k t -> b v k p n t")[bass.ds(b, 1), 2 * e + h, m]
                            sp.dma_start(dst.rearrange("o p n t -> p (o n) t"), t[:, m % 2, e, :].bitcast(F32).rearrange(
                                "p (n t) -> p n t", n=N)).then_inc(stored[m % 2], 16)

            def body(b, first, last):
                if not first:
                    store(b - 1)
                if not last:
                    sp.wait_ge(projected, b * 8 + 8)
                    sp.wait_ge(v_full, b * 4 + 4)
                    load_s(b + 1)

            for i in range(2):
                sp.sem_inc(stored[i], 64)
            load_s(0)
            for i in range(NP):
                if i >= TR:
                    sp.wait_ge(w_split, i - TR + 1)
                sp.dma_start(wraw[:, i % TR, :], g.w_pieces[PC_ATT + i]).then_inc(w_loaded[i % TR], 16)
            blocks(sp, body)
            store(NB - 1)
            for i in range(2):
                sp.wait_ge(stored[i], 64 * (2 * NB + 1))

        @block.scalar
        def _(act):
            def q_evac(b, m):
                act.wait_ge(projected, b * 8 + (2 * m + 1))
                if not isinstance(b, int) or 4 * b + m >= 2:
                    act.wait_ge(scored, b * 8 + (2 * m - 2))
                for e in range(2):
                    act.activation(qk[:, m % 2, e, :], b_qk[:, 0, e * C:(e + 1) * C], ACT.Identity,
                                   bias=bcol(M_Q + e, m)).then_inc(q_read, 1)

            def square(b, m, h):
                act.wait_ge(scored, b * 8 + (2 * m + h + 1))
                act.wait_ge(step, b * 32 + 8 * m)
                act.activation(sq[:, h, :], b_sc[:, h, :], ACT.Square).then_inc(squared, 1)

            def pt_evac(b, m):
                act.wait_ge(p_turned, b * 4 + (m + 1))
                if not isinstance(b, int) or 4 * b + m >= 2:
                    act.wait_ge(mixed, b * 4 + (m - 1))
                act.activation(ptl[:, m % 2, :], b_pt[:, m % 2, :], ACT.Copy).then_inc(pt_read, 1)

            def o_high(b, m):
                act.wait_ge(mixed, b * 4 + (m + 1))
                for e in range(2):
                    act.activation(ohi[:, m, e, :], b_mx[:, m % 2, e * C:(e + 1) * C], ACT.Identity,
                                   bias=bcol(M_V + e, m)).then_inc(o_hi, 1)

            def a_high(b, m):
                act.wait_ge(wo_full, b * 4 + (m + 1))
                act.wait_ge(stored[m % 2], b * 128 + 64 * (m // 2 + 1))
                for e in range(2):
                    act.activation(by_state(ahi[:, m % 2, e, :]), by_group(b_qk[:, m % 2, e * C:(e + 1) * C]), ACT.Identity,
                                   bias=bcol(M_O + e, m)).then_inc(a_hi, 1)

            def before(b, m):
                return (b, m - 1) if m else (b - 1, KD - 1)

            def body(b, first, last):
                for m in range(KD):
                    if m < KD - 1:
                        q_evac(b, m + 1)
                    if not (first and m == 0):
                        pt_evac(*before(b, m))
                    square(b, m, 0)
                    square(b, m, 1)
                    act.wait_ge(step, b * 32 + (8 * m + 3))
                    act.activation(sc[:, 1, :, :], sc[:, 0, :, :], ACT.Sqrt, scale=1.0 / HD,
                                   bias=g.tiny_hd[:, :]).then_inc(mag_done, 1)
                    act.wait_ge(step, b * 32 + (8 * m + 5))
                    act.activation(sc[:, 4, :, :], sc[:, 3, :, :], ACT.Exp).then_inc(exp_done, 1)
                    if not (first and m == 0):
                        o_high(*before(b, m))
                    if m == 0:
                        for i in range(2 * NG):
                            act.wait_ge(v_full, b * 4 + (i + 1))
                            act.activation(v[:, i // 2, i % 2, :], b_qk[:, i % 2, :], ACT.Copy).then_inc(v_read, 1)
                        if not first:
                            for mm in range(KD):
                                a_high(b - 1, mm)
                if not last:
                    q_evac(b + 1, 0)

            for i in range(NP):
                act.wait_ge(w_loaded[i % TR], 16 * (i // TR + 1))
                act.activation(whi[:, i, :], wraw[:, i % TR, :], ACT.Copy).then_inc(w_hi, 1)
            q_evac(0, 0)
            blocks(act, body)
            pt_evac(NB - 1, KD - 1)
            o_high(NB - 1, KD - 1)
            for m in range(KD):
                a_high(NB - 1, m)

        @block.vector
        def _(dve):
            def k_evac(b, m):
                dve.wait_ge(projected, b * 8 + (2 * m + 2))
                if not isinstance(b, int) or 4 * b + m >= 2:
                    dve.wait_ge(scored, b * 8 + (2 * m - 2))
                for e in range(2):
                    dve.tensor_scalar(qk[:, m % 2, 2 + e, :], b_qk[:, 1, e * C:(e + 1) * C], bcol(M_K + e, m), None,
                                      ALU.add).then_inc(k_read, 1)
                dve.tensor_scalar(qk[:, m % 2, 4, :], b_qk[:, 1, C:2 * C], bcol(M_K + 1, m), -1.0,
                                  ALU.add, ALU.mult).then_inc(k_read, 1)

            def softmax(b, m):
                done = [0]

                def link(ins):
                    ins.then_inc(step, 1)
                    done[0] += 1
                    dve.wait_ge(step, b * 32 + (8 * m + done[0]))

                dve.wait_ge(squared, b * 8 + (2 * m + 2))
                sqv = sq[:, :, :].rearrange("p h (a c) -> p a h c", a=2)
                link(dve.tensor_tensor(m2[:, :].rearrange("p (h c) -> p h c", h=2), sqv[:, 0], sqv[:, 1], ALU.add))
                sqv = m2[:, :].rearrange("p (g c) -> p g c", g=GH)
                mask = g.mask[:, :, :].rearrange("p n b -> p (n b)").unsqueeze(1).to_broadcast([P, GH, P])
                link(dve.tensor_tensor(sqv, sqv, mask, ALU.mult))
                link(dve.tensor_reduce(sc[:, 0, :, :].rearrange("p g n -> p (g n)"),
                                       m2[:, :].rearrange("p (x b) -> p x b", b=GB), AX.X, ALU.add))
                dve.wait_ge(mag_done, b * 4 + (m + 1))
                link(dve.tensor_reduce(sc[:, 2, :, 0], sc[:, 1, :, :], AX.X, ALU.max))
                link(dve.tensor_tensor(sc[:, 3, :, :], sc[:, 1, :, :],
                                       sc[:, 2, :, 0:1].to_broadcast([P, GH, N]), ALU.subtract))
                dve.wait_ge(exp_done, b * 4 + (m + 1))
                link(dve.tensor_reduce(sc[:, 2, :, 1], sc[:, 4, :, :], AX.X, ALU.add))
                link(dve.reciprocal(sc[:, 2, :, 2], sc[:, 2, :, 1]))
                for x in range(GH):
                    dve.wait_ge(p_turned, b * 4 + m) if x == 0 else None
                    ins = dve.scalar_tensor_tensor(
                        out=pd[:, x, :, :], in0=sc[:, 4, x, :].unsqueeze(2).to_broadcast([P, N, GB]),
                        scalar=sc[:, 2, x, 2:3], in1=g.mask[:, :, :], op0=ALU.mult, op1=ALU.mult)
                ins.then_inc(step, 1)

            def o_low(b, m):
                dve.wait_ge(o_hi, b * 8 + (2 * m + 2))
                for e in range(2):
                    dve.scalar_tensor_tensor(out=olo[:, m, e, :], in0=b_mx[:, m % 2, e * C:(e + 1) * C],
                                             scalar=bcol(M_V + e, m), in1=ohi[:, m, e, :].bitcast(F32),
                                             op0=ALU.add, op1=ALU.subtract).then_inc(o_split, 1)

            def a_low(b, m):
                dve.wait_ge(stored[m % 2], b * 128 + 64 * (m // 2 + 1))
                dve.wait_ge(a_hi, b * 8 + (2 * m + 2))
                for e in range(2):
                    for gr in range(NG):
                        ins = dve.scalar_tensor_tensor(
                            out=by_state(alo[:, m % 2, e, :])[:, gr], in0=by_group(b_qk[:, m % 2, e * C:(e + 1) * C])[:, gr],
                            scalar=bcol(M_O + e, m), in1=by_state(ahi[:, m % 2, e, :].bitcast(F32))[:, gr],
                            op0=ALU.add, op1=ALU.subtract)
                    ins.then_inc(a_split, 1)

            def before(b, m):
                return (b, m - 1) if m else (b - 1, KD - 1)

            def body(b, first, last):
                for m in range(KD):
                    if m < KD - 1:
                        k_evac(b, m + 1)
                    softmax(b, m)
                    if not (first and m == 0):
                        o_low(*before(b, m))
                    if m == 0 and not first:
                        for mm in range(KD):
                            a_low(b - 1, mm)
                if not last:
                    k_evac(b + 1, 0)

            for i in range(NP):
                dve.wait_ge(w_hi, i + 1)
                dve.tensor_tensor(wlo[:, i, :], wraw[:, i % TR, :], whi[:, i, :].bitcast(F32),
                                  ALU.subtract).then_inc(w_split, 1)
            k_evac(0, 0)
            blocks(dve, body)
            o_low(NB - 1, KD - 1)
            for m in range(KD):
                a_low(NB - 1, m)

        @block.tensor
        def _(pe):
            def project(b, m):
                pe.wait_ge(s_loaded, b * 64 + 64)
                for i in range(2):
                    pe.wait_ge(w_split, (M_Q, M_K)[i] * KD + 2 * KD)
                    pe.wait_ge((q_read, k_read)[i], (b * 4 + m) * (2, 3)[i])
                    if m == 0:
                        pe.wait_ge(a_split, b * 8 - 8 if not isinstance(b, int) else max(b * 8 - 8, 0))
                    if m == 2:
                        pe.wait_ge(v_read, b * 4 + 4)
                        pe.wait_ge(a_split, b * 8)
                    for e in range(2):
                        for k in range(KD):
                            w = ((M_Q, M_K)[i] + e) * KD + k
                            mm = split3(pe.matmul, b_qk[:, i, e * C:(e + 1) * C], whi[:, w, m * P:(m + 1) * P],
                                        wlo[:, w, m * P:(m + 1) * P], sx[:, e, 0, :, k, :], sx[:, e, 1, :, k, :],
                                        k == 0, k == KD - 1)
                    mm.then_inc(projected, 1)

            def values(b):
                pe.wait_ge(w_split, M_O * KD)
                for i in range(2 * NG):
                    gr, e = i // 2, i % 2
                    if i < 2:
                        pe.wait_ge((q_read, k_read)[i], (b * 4 + 2) * (2, 3)[i])
                    else:
                        pe.wait_ge(v_read, b * 4 + (i - 1))
                    for k in range(KD):
                        w = (M_V + e) * KD + k
                        mm = split3(pe.matmul, b_qk[:, i % 2, :], sx[:, e, 0, gr, k, :], sx[:, e, 1, gr, k, :],
                                    whi[:, w, :], wlo[:, w, :], k == 0, k == KD - 1)
                    mm.then_inc(v_full, 1)

            def score(b, m, gr):
                if gr == 0:
                    pe.wait_ge(q_read, b * 8 + (2 * m + 2))
                    pe.wait_ge(k_read, b * 12 + (3 * m + 3))
                    pe.wait_ge(squared, b * 8 + 2 * m)
                cols = slice(gr * P, (gr + 1) * P)
                for part, pairs in enumerate((((0, 2), (1, 3)), ((1, 2), (0, 4)))):
                    for n, (q, k) in enumerate(pairs):
                        for h in range(2):
                            hp = slice(h * HD, (h + 1) * HD)
                            mm = pe.matmul(b_sc[:, h, (part * NG + gr) * P:(part * NG + gr + 1) * P],
                                           qk[hp, m % 2, q, cols], qk[hp, m % 2, k, cols], start=n == 0, stop=n == 1)
                            if gr == NG - 1 and part == 1 and n == 1:
                                mm.then_inc(scored, 1)

            def turn(b, m):
                pe.wait_ge(step, b * 32 + (8 * m + 8))
                for x in range(GH):
                    mm = pe.transpose(b_pt[:, m % 2, x * P:(x + 1) * P],
                                      pd[:, x, :, :].rearrange("p n b -> p (n b)"), g.ident[:, :])
                mm.then_inc(p_turned, 1)

            def mix(b, m):
                pe.wait_ge(pt_read, b * 4 + (m + 1))
                pe.wait_ge(v_read, b * 4 + 4)
                if not isinstance(b, int) or 4 * b + m >= 2:
                    pe.wait_ge(o_split, b * 8 + (2 * m - 2))
                for gr, e, h in [(gr, e, h) for gr in range(NG) for e in range(2) for h in range(2)]:
                    x = h * NG + gr
                    if True:
                        out = b_mx[h * HD:(h + 1) * HD, m % 2, e * C + gr * P:e * C + (gr + 1) * P]
                        mm = pe.matmul(out, v[:, gr, e, (2 * m + h) * HD:(2 * m + h + 1) * HD],
                                       ptl[:, m % 2, x * P:(x + 1) * P],
                                       start=True, stop=True)
                mm.then_inc(mixed, 1)

            def project_out(b, alone=False):
                pe.wait_ge(w_split, NP)
                pe.wait_ge(o_split, b * 8 + 8)
                for m in range(KD):
                    if m < 2 and alone:
                        pe.wait_ge((q_read, k_read)[m], NB * 4 * (2, 3)[m])
                    elif m < 2:
                        pe.wait_ge(v_read, b * 4 + (4 + 3 + m))
                    else:
                        pe.wait_ge(a_split, b * 8 + (2 * m - 2))
                    for e in range(2):
                        for k in range(KD):
                            w = (M_O + e) * KD + k
                            mm = split3(pe.matmul, b_qk[:, m % 2, e * C:(e + 1) * C], whi[:, w, m * P:(m + 1) * P],
                                        wlo[:, w, m * P:(m + 1) * P], ohi[:, k, e, :], olo[:, k, e, :],
                                        k == 0, k == KD - 1)
                    mm.then_inc(wo_full, 1)

            def before(b, m):
                return (b, m - 1) if m else (b - 1, KD - 1)

            def body(b, first, last):
                for m in range(KD):
                    if m < KD - 1:
                        project(b, m + 1)
                    score(b, m, 0)
                    if not (first and m == 0):
                        turn(*before(b, m))
                    score(b, m, 1)
                    if not (first and m == 0):
                        mix(*before(b, m))
                    if m == 0:
                        values(b)
                        if not first:
                            project_out(b - 1)
                if not last:
                    project(b + 1, 0)

            project(0, 0)
            blocks(pe, body)
            turn(NB - 1, KD - 1)
            mix(NB - 1, KD - 1)
            project_out(NB - 1, True)


def phase_interfere(nc, g):
    s = Stage(nc, "i")
    NP = 2 * N * KD
    TR = 2
    LEAST = 1e-34
    PAIRS = [(i, j) for i in range(N) for j in range(i + 1, N)]
    with s.ctx:
        stage = s.sb("stage", [P, 4, W])
        whi = s.sb("whi", [P, NP, W], F32R)
        wlo = s.sb("wlo", [P, NP, W], F32R)
        ax = s.sb("ax", [P, 2, 4, KD, P], F32R)
        ng = s.sb("ng", [P, 2, 2, KD, P], F32R)
        mag = s.sb("mag", [P, N, W])
        inv = s.sb("inv", [P, N, W])
        cs = s.sb("cs", [P, 2, N, W])
        zero = s.sb("zero", [P, N, W], BF16)
        t1 = s.sb("t1", [P, W])
        t2 = s.sb("t2", [P, W])
        sup = s.sb("sup", [P, 2, W])
        ids = s.sb("ids", [P, TT, N], mybir.dt.int32)
        emb = s.sb("emb", [P, TT, N * N])
        st = s.sb("st", [P, N * N])
        nrm = s.sb("nrm", [P, 3])
        w_loaded = [s.sem(f"w_loaded{i}") for i in range(TR)]
        w_hi = s.sem("w_hi")
        w_split = s.sem("w_split")
        ids_in = s.sem("ids_in")
        emb_in = s.sem("emb_in")
        a_loaded = [s.sem(f"a_loaded{i}") for i in range(2)]
        a_used = s.sem("a_used")
        negated = s.sem("negated")
        multiplied = s.sem("multiplied")
        squared = s.sem("squared")
        summed = s.sem("summed")
        mag_done = s.sem("mag_done")
        unit = s.sem("unit")
        chain = s.sem("chain")
        sup_done = s.sem("sup_done")
        len_done = s.sem("len_done")
        len_inv = s.sem("len_inv")
        scaled = s.sem("scaled")
        stored = s.sem("stored")
        block = s.ctx.enter_context(nc.Block())

        @block.sync
        def _(sp):
            def load(t, n):
                sp.wait_ge(a_used, t * N + (n + 1))
                for half in range(P // BT):
                    src = g.a_scr[bass.ds(t * (P // BT) + half, 1), n].rearrange("o p v k t -> p (o v k) t")
                    sp.dma_start(ax[:, n % 2, :, :, half * BT:(half + 1) * BT].bitcast(F32).rearrange(
                        "p v k t -> p (v k) t"), src).then_inc(a_loaded[n % 2], 16)

            def store(t):
                sp.wait_ge(scaled, t + 1)
                sp.dma_start(g.sup_scr[bass.ds(t, 1)].rearrange("o p a n -> p (o a n)"),
                             sup[:, :, :].rearrange("p a n -> p (a n)")).then_inc(stored, 16)

            sp.dma_start(ids[:, :, :], g.ids.rearrange("(t p) f -> p t f", p=P)).then_inc(ids_in, 16)
            load(0, 0)
            load(0, 1)
            for i in range(NP):
                if i >= TR:
                    sp.wait_ge(w_split, i - TR + 1)
                sp.dma_start(stage[:, i % TR, :], g.w_pieces[PC_INT + i]).then_inc(w_loaded[i % TR], 16)
            load(0, 2)
            load(0, 3)
            with sp.Fori(1, TT) as t:
                for n in range(N):
                    load(t, n)
                store(t - 1)
            store(TT - 1)
            sp.wait_ge(stored, 16 * TT)

        @block.gpsimd
        def _(pool):
            pool.wait_ge(ids_in, 16)
            for t in range(TT):
                for f, tbl in enumerate((g.tbl_0, g.tbl_1, g.tbl_2, g.tbl_3)):
                    pool.indirect_dma_start(
                        out=emb[:, t, f * N:(f + 1) * N], out_offset=None, in_=tbl,
                        in_offset=bass.IndirectOffsetOnAxis(ap=ids[:, t, f:f + 1].bitcast(U32), axis=0)).then_inc(emb_in, 16)
            with pool.Fori(0, TT) as t:
                for n in range(N):
                    pool.wait_ge(a_loaded[n % 2], t * 64 + (n // 2) * 32 + 32)
                    pool.wait_ge(a_used, t * N + (n + 1))
                    for h in range(2):
                        pool.tensor_tensor(ng[:, n % 2, h, :, :].rearrange("p k t -> p (k t)"),
                                           g.none[:, :].to_broadcast([P, KD * P]),
                                           ax[:, n % 2, 2 + h, :, :].bitcast(F32).rearrange("p k t -> p (k t)"),
                                           ALU.subtract).then_inc(negated, 1)

        @block.scalar
        def _(act):
            def squares(t, n):
                for part in range(2):
                    act.wait_ge(multiplied, t * 8 + (2 * n + 2))
                    if not isinstance(t, int) or 4 * t + n >= 2:
                        act.wait_ge(summed, t * N + (n - 1))
                    act.activation(stage[:, 2 * (n % 2) + part, :], g.ps[:, part * N + n, :],
                                   ACT.Square).then_inc(squared, 1)

            def magnitude(t, n):
                act.wait_ge(summed, t * N + (n + 1))
                act.activation(mag[:, n, :], mag[:, n, :], ACT.Sqrt).then_inc(mag_done, 1)

            def length(t):
                act.wait_ge(sup_done, t + 1)
                act.activation(cs[:, 0, 0:2, :], sup[:, :, :], ACT.Square, accum_out=nrm[:, 0:1]).then_inc(len_done, 1)
                act.wait_ge(len_done, t * 2 + 1)
                act.activation(nrm[:, 1:2], nrm[:, 0:1], ACT.Sqrt, bias=g.tiny[:, :]).then_inc(len_done, 1)

            def scale(t):
                act.wait_ge(len_inv, t + 1)
                act.activation(sup[:, :, :], sup[:, :, :], ACT.Copy, scale=nrm[:, 2:3]).then_inc(scaled, 1)

            for i in range(NP):
                act.wait_ge(w_loaded[i % TR], 16 * (i // TR + 1))
                act.activation(whi[:, i, :], stage[:, i % TR, :], ACT.Copy).then_inc(w_hi, 1)
            act.wait_ge(w_split, NP)

            def body(t, first):
                squares(t, 0)
                squares(t, 1)
                magnitude(t, 0)
                if not first:
                    scale(t - 1)
                squares(t, 2)
                magnitude(t, 1)
                squares(t, 3)
                magnitude(t, 2)
                magnitude(t, 3)
                length(t)

            body(0, True)
            with act.Fori(1, TT) as t:
                body(t, False)
            scale(TT - 1)

        @block.vector
        def _(dve):
            for i in range(NP):
                dve.wait_ge(w_hi, i + 1)
                dve.tensor_tensor(wlo[:, i, :], stage[:, i % TR, :], whi[:, i, :].bitcast(F32),
                                  ALU.subtract).then_inc(w_split, 1)
            dve.wait_ge(emb_in, 16 * TT * N)

            def body(t, first):
                done = [0]

                def link(ins):
                    ins.then_inc(chain, 1)
                    done[0] += 1
                    dve.wait_ge(chain, t * CHAIN_STEPS + done[0])

                def add_squares(n):
                    dve.wait_ge(squared, t * 8 + (2 * n + 2))
                    link(dve.tensor_tensor(mag[:, n, :], stage[:, 2 * (n % 2), :], stage[:, 2 * (n % 2) + 1, :], ALU.add))
                    dve.tensor_scalar(zero[:, n, :], mag[:, n, :], LEAST, None, ALU.is_lt)
                    dve.tensor_scalar(mag[:, n, :], mag[:, n, :], LEAST, None, ALU.max).then_inc(summed, 1)

                def unit_vector(n):
                    dve.wait_ge(mag_done, t * N + (n + 1))
                    link(dve.reciprocal(inv[:, n, :], mag[:, n, :]))
                    for part in range(2):
                        dve.tensor_tensor(cs[:, part, n, :], g.ps[:, part * N + n, :], inv[:, n, :], ALU.mult).then_inc(unit, 1)

                def inverse_length(b):
                    dve.wait_ge(len_done, b * 2 + 2)
                    dve.reciprocal(nrm[:, 2:3], nrm[:, 1:2]).then_inc(len_inv, 1)

                add_squares(0)
                if not first:
                    inverse_length(t - 1)
                add_squares(1)
                unit_vector(0)
                add_squares(2)
                unit_vector(1)
                add_squares(3)
                unit_vector(2)
                link(dve.tensor_copy(st[:, :], emb[:, bass.ds(t, 1), :].rearrange("p o x -> p (o x)")))
                unit_vector(3)
                dve.wait_ge(unit, t * 8 + 16)
                w = inv
                seen = set()
                for i, j in PAIRS:
                    dve.tensor_tensor(t1[:, :], cs[:, 0, i, :], cs[:, 0, j, :], ALU.mult)
                    link(dve.tensor_tensor(t2[:, :], cs[:, 1, i, :], cs[:, 1, j, :], ALU.mult))
                    link(dve.tensor_tensor(t1[:, :], t1[:, :], t2[:, :], ALU.add))
                    link(dve.tensor_tensor(t2[:, :], zero[:, i, :], zero[:, j, :], ALU.add))
                    link(dve.tensor_tensor(t1[:, :], t1[:, :], t2[:, :], ALU.add))
                    for a, b in ((i, j), (j, i)):
                        e = st[:, a * N + b:a * N + b + 1]
                        if b in seen:
                            ins = dve.scalar_tensor_tensor(out=w[:, b, :], in0=t1[:, :], scalar=e, in1=w[:, b, :],
                                                           op0=ALU.mult, op1=ALU.add)
                        else:
                            ins = dve.tensor_scalar(w[:, b, :], t1[:, :], e, st[:, b * N + b:b * N + b + 1],
                                                    ALU.mult, ALU.add)
                            seen.add(b)
                    link(ins)
                link(dve.tensor_tensor(w[:, :, :], w[:, :, :], mag[:, :, :], ALU.mult))
                for part in range(2):
                    ins = dve.tensor_tensor(cs[:, part, :, :], cs[:, part, :, :], w[:, :, :], ALU.mult)
                link(ins)
                ins = dve.tensor_tensor(cs[:, :, 0:2, :], cs[:, :, 0:2, :], cs[:, :, 2:4, :], ALU.add)
                link(ins)
                dve.wait_ge(stored, t * 16)
                dve.tensor_tensor(sup[:, :, :], cs[:, :, 0, :], cs[:, :, 1, :], ALU.add).then_inc(sup_done, 1)
                assert done[0] == CHAIN_STEPS

            CHAIN_STEPS = 4 + 4 + 1 + 5 * len(PAIRS) + 3
            body(0, True)
            with dve.Fori(1, TT) as t:
                body(t, False)
            dve.wait_ge(len_done, 2 * TT)
            dve.reciprocal(nrm[:, 2:3], nrm[:, 1:2]).then_inc(len_inv, 1)

        @block.tensor
        def _(pe):
            pe.sem_inc(a_used, 2)
            pe.sem_inc(unit, 2 * N)
            with pe.Fori(0, TT) as t:
                for n in range(N):
                    pe.wait_ge(w_split, (n + 1) * 2 * KD)
                    pe.wait_ge(a_loaded[n % 2], t * 64 + (n // 2) * 32 + 32)
                    pe.wait_ge(negated, t * 8 + (2 * n + 2))
                    pe.wait_ge(unit, t * 8 + (2 * n + 2))
                    for part in range(2):
                        for x in range(2):
                            for k in range(KD):
                                w = (2 * n + (x if part == 0 else 1 - x)) * KD + k
                                a = ax[:, n % 2, :, k, :]
                                hi, lo = ((a[:, 0], a[:, 1]), (ng[:, n % 2, 0, k, :], ng[:, n % 2, 1, k, :]) if part == 0
                                          else (a[:, 2], a[:, 3]))[x]
                                mm = split3(pe.matmul, g.ps[:, part * N + n, :], hi, lo, whi[:, w, :], wlo[:, w, :],
                                            x == 0 and k == 0, x == 1 and k == KD - 1)
                        mm.then_inc(multiplied, 1)
                    pe.drain().then_inc(a_used, 1)


def phase_top(nc, g):
    s = Stage(nc, "e")
    R = 256
    NB, NT = TOK // R, R // P
    NP, TR = N_TOP, 2
    W_MR, W_MI, W_POST, W_T1, W_T2 = 0, KD, 2 * KD, 3 * KD, 4 * KD
    with s.ctx:
        wraw = s.sb("wraw", [P, TR, W])
        whi = s.sb("whi", [P, NP, W], F32R)
        wlo = s.sb("wlo", [P, NP, W], F32R)
        row = s.sb("row", [P, 2 * W])
        sup = s.sb("sup", [P, NT, 2, KD, P])
        shi = s.sb("shi", [P, 2, KD, R], F32R)
        slo = s.sb("slo", [P, 2, KD, R], F32R)
        nhi = s.sb("nhi", [P, KD, R], F32R)
        nlo = s.sb("nlo", [P, KD, R], F32R)
        sqm = s.sb("sqm", [P, 2, R])
        amp = s.sb("amp", [P, KD, R])
        ahi = s.sb("ahi", [P, KD, R], F32R)
        alo = s.sb("alo", [P, KD, R], F32R)
        u = s.sb("u", [P, NT, W])
        ust = s.sb("ust", [P, NT, 6])
        umv = s.sb("umv", [P, NT, 2])
        usd = s.sb("usd", [P, NT])
        uri = s.sb("uri", [P, NT])
        z = s.sb("z", [P, KD, R])
        zhi = s.sb("zhi", [P, KD, R], F32R)
        zlo = s.sb("zlo", [P, KD, R], F32R)
        tx = s.sb("tx", [P, NT, W])
        r = s.sb("r", [P, KD, R])
        rhi = s.sb("rhi", [P, KD, R], F32R)
        rlo = s.sb("rlo", [P, KD, R], F32R)
        yt = s.sb("yt", [P, NT, TOP2])
        yj = s.sb("yj", [P, NT, TOP2])
        y2 = s.sb("y2", [P, NT])
        y = s.sb("y", [P, TT])
        w_loaded = [s.sem(f"w_loaded{i}") for i in range(TR)]
        row_in, w_hi, w_split = s.sem("row_in"), s.sem("w_hi"), s.sem("w_split")
        sup_in, tx_in = s.sem("sup_in"), s.sem("tx_in")
        s_turned = s.sem("s_turned")
        s_hi, s_split = s.sem("s_hi"), s.sem("s_split")
        negated = s.sem("negated")
        measured = s.sem("measured")
        m_squared = s.sem("m_squared")
        m_summed = s.sem("m_summed")
        amp_done = s.sem("amp_done")
        a_hi, a_split = s.sem("a_hi"), s.sem("a_split")
        posted = s.sem("posted")
        u_read = s.sem("u_read")
        u_step = s.sem("u_step")
        sd_done = s.sem("sd_done")
        u_ready = s.sem("u_ready")
        z_turned = s.sem("z_turned")
        z_done = s.sem("z_done")
        z_hi, z_split = s.sem("z_hi"), s.sem("z_split")
        top1 = s.sem("top1")
        t1_read = s.sem("t1_read")
        r_turned = s.sem("r_turned")
        r_done = s.sem("r_done")
        r_hi, r_split = s.sem("r_hi"), s.sem("r_split")
        top2 = s.sem("top2")
        y_step = s.sem("y_step")
        y_done = s.sem("y_done")
        out_done = s.sem("out_done")
        block = s.ctx.enter_context(nc.Block())

        def pipeline(eng, body):
            body(0, None)
            body(1, 0)
            with eng.Fori(2, NB) as t:
                body(t, t - 1)
            body(None, NB - 1)

        def flat(t):
            return t.rearrange("p k n -> p (k n)")

        @block.sync
        def _(sp):
            def body(t):
                sp.wait_ge(s_turned, t * 4)
                sp.dma_start(sup[:, :, :, :, :].rearrange("p t a k n -> p t (a k n)"),
                             g.sup_scr[bass.ds(t * NT, NT)].rearrange("t p a n -> p t (a n)")).then_inc(sup_in, 16)
                sp.wait_ge(r_turned, t * 2)
                sp.dma_start(tx[:, :, :], g.h_scr[CHUNKS_A - 1, bass.ds(t * NT, NT)].rearrange(
                    "t p n -> p t n")).then_inc(tx_in, 16)

            sp.dma_start(row[:, :], g.row2.rearrange("o n -> (o n)").partition_broadcast(P)).then_inc(row_in, 16)
            for i in range(NP):
                if i >= TR:
                    sp.wait_ge(w_split, i - TR + 1)
                sp.dma_start(wraw[:, i % TR, :], g.w_pieces[PC_TOP + i]).then_inc(w_loaded[i % TR], 16)
            body(0)
            with sp.Fori(1, NB) as t:
                body(t)
            sp.wait_ge(y_done, NB)
            sp.dma_start(g.out.rearrange("(t p) o -> p (t o)", p=P), y[:, :], allow_slow_non_contiguous=True).then_inc(out_done, 16)
            sp.wait_ge(out_done, 16)

        @block.gpsimd
        def _(pool):
            def negate(t):
                pool.wait_ge(s_split, t * 4 + 4)
                pool.wait_ge(measured, t * 4)
                for n, x in ((nhi, shi), (nlo, slo)):
                    pool.tensor_tensor(flat(n), g.none[:, :].to_broadcast([P, KD * R]), flat(x[:, 1].bitcast(F32)),
                                       ALU.subtract).then_inc(negated, 1)

            negate(0)
            with pool.Fori(1, NB) as t:
                negate(t)

        @block.scalar
        def _(act):
            def sup_high(t):
                for q in range(4):
                    act.wait_ge(s_turned, t * 4 + (q + 1))
                    act.wait_ge(measured, t * 4)
                    act.activation(shi[:, q // 2, 2 * (q % 2):2 * (q % 2) + 2, :].rearrange("p k n -> p (k n)"),
                                   g.ps[:, q % 2, :], ACT.Copy).then_inc(s_hi, 1)

            def amplitude(t, m):
                act.wait_ge(measured, t * 4 + (m + 1))
                act.wait_ge(m_summed, t * 4 + m)
                act.activation(sqm[:, :, :].rearrange("p a n -> p (a n)"), g.ps[:, 2 + m % 2, :],
                               ACT.Square).then_inc(m_squared, 1)
                act.wait_ge(m_summed, t * 4 + (m + 1))
                act.activation(amp[:, m, :], amp[:, m, :], ACT.Sqrt).then_inc(amp_done, 1)
                act.wait_ge(amp_done, t * 4 + (m + 1))
                act.wait_ge(posted, t * 2)
                act.activation(ahi[:, m, :], amp[:, m, :], ACT.Copy).then_inc(a_hi, 1)

            def deviation(t):
                act.wait_ge(u_step, t * 4 + 3)
                act.activation(usd[:, :], umv[:, :, 1], ACT.Sqrt, bias=g.eps_ln[:, :]).then_inc(sd_done, 1)

            def gelu(t):
                for k in range(KD):
                    act.wait_ge(z_turned, t * 2 + (k // 2 + 1))
                    act.wait_ge(z_split, t)
                    act.activation(z[:, k, :], g.ps[:, 6 + k // 2, (k % 2) * R:(k % 2 + 1) * R], ACT.Gelu,
                                   bias=g.cols[:, COL_PBE + k:COL_PBE + k + 1],
                                   scale=g.cols[:, COL_PG + k:COL_PG + k + 1]).then_inc(z_done, 1)
                act.wait_ge(z_done, t * 4 + 4)
                act.wait_ge(top1, t * 2)
                act.activation(flat(zhi), flat(z), ACT.Copy).then_inc(z_hi, 1)

            def relu(t):
                for q in range(2):
                    act.wait_ge(r_turned, t * 2 + (q + 1))
                    act.wait_ge(r_split, t)
                    act.activation(r[:, 2 * q:2 * q + 2, :].rearrange("p k n -> p (k n)"), g.ps[:, 6 + q, :],
                                   ACT.Relu).then_inc(r_done, 1)
                act.wait_ge(r_done, t * 2 + 2)
                act.wait_ge(top2, t)
                act.activation(flat(rhi), flat(r), ACT.Copy).then_inc(r_hi, 1)

            for i in range(NP):
                act.wait_ge(w_loaded[i % TR], 16 * (i // TR + 1))
                act.activation(whi[:, i, :], wraw[:, i % TR, :], ACT.Copy).then_inc(w_hi, 1)

            def body(t1, t2):
                if t1 is not None:
                    sup_high(t1)
                if t2 is not None:
                    deviation(t2)
                if t1 is not None:
                    amplitude(t1, 0)
                    amplitude(t1, 1)
                if t2 is not None:
                    gelu(t2)
                if t1 is not None:
                    amplitude(t1, 2)
                    amplitude(t1, 3)
                if t2 is not None:
                    relu(t2)

            pipeline(act, body)

        @block.vector
        def _(dve):
            def sup_low(t):
                for q in range(4):
                    dve.wait_ge(s_hi, t * 4 + (q + 1))
                    if q == 0:
                        dve.wait_ge(negated, t * 2)
                    dve.tensor_tensor(slo[:, q // 2, 2 * (q % 2):2 * (q % 2) + 2, :].rearrange("p k n -> p (k n)"),
                                      g.ps[:, q % 2, :], shi[:, q // 2, 2 * (q % 2):2 * (q % 2) + 2, :].bitcast(F32).rearrange(
                                          "p k n -> p (k n)"), ALU.subtract).then_inc(s_split, 1)

            def amplitude(t, m):
                dve.wait_ge(m_squared, t * 4 + (m + 1))
                dve.tensor_tensor(amp[:, m, :], sqm[:, 0, :], sqm[:, 1, :], ALU.add).then_inc(m_summed, 1)
                dve.wait_ge(a_hi, t * 4 + (m + 1))
                dve.tensor_tensor(alo[:, m, :], amp[:, m, :], ahi[:, m, :].bitcast(F32), ALU.subtract).then_inc(a_split, 1)

            def post(t):
                for i in range(NT):
                    dve.wait_ge(posted, t * 2 + (i + 1))
                    if i == 0:
                        dve.wait_ge(z_turned, t * 2)
                    dve.tensor_tensor(u[:, i, :], g.ps[:, 4 + i, :], row[:, 0:W], ALU.add).then_inc(u_read, 1)
                dve.wait_ge(u_read, t * 2 + 2)
                for i in range(NT):
                    ins = dve.bn_stats(ust[:, i, :], u[:, i, :])
                ins.then_inc(u_step, 1)
                dve.wait_ge(u_step, t * 4 + 1)
                dve.tensor_scalar(uri[:, :], ust[:, :, 1], 0.0, None, ALU.mult)
                for i in range(NT):
                    dve.bn_aggr(umv[:, i, :], ust[:, i, :]).then_inc(u_step, 1)
                dve.wait_ge(sd_done, t + 1)
                dve.reciprocal(uri[:, :], usd[:, :]).then_inc(u_step, 1)
                dve.wait_ge(u_step, t * 4 + 4)
                for i in range(NT):
                    ins = dve.tensor_scalar(u[:, i, :], u[:, i, :], umv[:, i, 0:1], uri[:, i:i + 1], ALU.subtract, ALU.mult)
                ins.then_inc(u_ready, 1)

            def z_low(t):
                dve.wait_ge(z_hi, t + 1)
                dve.tensor_tensor(flat(zlo), flat(z), flat(zhi).bitcast(F32), ALU.subtract).then_inc(z_split, 1)

            def add_rx(t):
                dve.wait_ge(tx_in, t * 16 + 16)
                for i in range(NT):
                    dve.wait_ge(top1, t * 2 + (i + 1))
                    dve.tensor_tensor(tx[:, i, :], g.ps[:, 4 + i, :], tx[:, i, :], ALU.add).then_inc(t1_read, 1)

            def r_low(t):
                dve.wait_ge(r_hi, t + 1)
                dve.tensor_tensor(flat(rlo), flat(r), flat(rhi).bitcast(F32), ALU.subtract).then_inc(r_split, 1)

            def output(t):
                dve.wait_ge(top2, t + 1)
                dve.tensor_tensor(yt[:, :, :], g.ps[:, 4, :].rearrange("p (t n) -> p t n", t=NT),
                                  row[:, W:W + TOP2].unsqueeze(1).to_broadcast([P, NT, TOP2]), ALU.add).then_inc(y_step, 1)
                dve.wait_ge(y_step, t * 3 + 1)
                for i in range(NT):
                    dve.scalar_tensor_tensor(out=yj[:, i, :], in0=yt[:, i, :], scalar=0.0, in1=row[:, W + TOP2:2 * W],
                                             op0=ALU.max, op1=ALU.mult, accum_out=y2[:, i:i + 1]).then_inc(y_step, 1)
                dve.wait_ge(y_step, t * 3 + 3)
                dve.tensor_copy(y[:, bass.ds(t * NT, NT)], y2[:, :]).then_inc(y_done, 1)

            for i in range(NP):
                dve.wait_ge(w_hi, i + 1)
                dve.tensor_tensor(wlo[:, i, :], wraw[:, i % TR, :], whi[:, i, :].bitcast(F32),
                                  ALU.subtract).then_inc(w_split, 1)
            dve.wait_ge(row_in, 16)

            def body(t1, t2):
                if t1 is not None:
                    sup_low(t1)
                if t2 is not None:
                    post(t2)
                if t1 is not None:
                    amplitude(t1, 0)
                    amplitude(t1, 1)
                if t2 is not None:
                    z_low(t2)
                if t1 is not None:
                    amplitude(t1, 2)
                if t2 is not None:
                    add_rx(t2)
                if t1 is not None:
                    amplitude(t1, 3)
                if t2 is not None:
                    r_low(t2)
                    output(t2)

            pipeline(dve, body)

        @block.tensor
        def _(pe):
            def turn_sup(t):
                pe.wait_ge(sup_in, t * 16 + 16)
                for q in range(4):
                    pe.wait_ge(s_split, t * 4 + 2 * (q // 2))
                    for k in (2 * (q % 2), 2 * (q % 2) + 1):
                        for i in range(NT):
                            mm = pe.transpose(g.ps[:, q % 2, (k % 2) * R + i * P:(k % 2) * R + (i + 1) * P],
                                              sup[:, i, q // 2, k, :], g.ident[:, :])
                    mm.then_inc(s_turned, 1)

            def measure(t, m):
                pe.wait_ge(w_split, W_POST)
                pe.wait_ge(s_split, t * 4 + 4)
                pe.wait_ge(negated, t * 2 + 2)
                if not isinstance(t, int) or 4 * t + m >= 2:
                    pe.wait_ge(m_squared, t * 4 + (m - 1))
                mc = slice(m * P, (m + 1) * P)
                for part in range(2):
                    terms = (((W_MR, shi[:, 0], slo[:, 0]), (W_MI, nhi, nlo)) if part == 0 else
                             ((W_MI, shi[:, 0], slo[:, 0]), (W_MR, shi[:, 1], slo[:, 1])))
                    for x, (w, hi, lo) in enumerate(terms):
                        for k in range(KD):
                            mm = split3(pe.matmul, g.ps[:, 2 + m % 2, part * R:(part + 1) * R], whi[:, w + k, mc],
                                        wlo[:, w + k, mc], hi[:, k, :], lo[:, k, :], x == 0 and k == 0,
                                        x == 1 and k == KD - 1)
                mm.then_inc(measured, 1)

            def rows_layer(bank, cols, hi, lo, piece, i, width=W, offset=0):
                for k in range(KD):
                    if width == W:
                        wh, wl = whi[:, piece + k, :], wlo[:, piece + k, :]
                    else:
                        c = slice((k % 2) * width, (k % 2 + 1) * width)
                        wh, wl = whi[:, piece + k // 2, c], wlo[:, piece + k // 2, c]
                    mm = split3(pe.matmul, g.ps[:, bank, cols], hi[:, k, i * P:(i + 1) * P], lo[:, k, i * P:(i + 1) * P],
                                wh, wl, k == 0, k == KD - 1)
                return mm

            def post(t):
                pe.wait_ge(w_split, W_T1)
                pe.wait_ge(a_split, t * 4 + 4)
                pe.wait_ge(t1_read, t * 2)
                pe.wait_ge(y_step, t * 3)
                for i in range(NT):
                    rows_layer(4 + i, slice(0, W), ahi, alo, W_POST, i).then_inc(posted, 1)

            def turn(src, bank, done):
                for q in range(2):
                    for k in (2 * q, 2 * q + 1):
                        for i in range(NT):
                            mm = pe.transpose(g.ps[:, bank + q, (k % 2) * R + i * P:(k % 2) * R + (i + 1) * P],
                                              src[:, i, k * P:(k + 1) * P], g.ident[:, :])
                    mm.then_inc(done, 1)

            def turn_z(t):
                pe.wait_ge(u_ready, t + 1)
                pe.wait_ge(r_done, t * 2)
                turn(u, 6, z_turned)

            def top_one(t):
                pe.wait_ge(w_split, W_T2)
                pe.wait_ge(z_split, t + 1)
                pe.wait_ge(u_read, t * 2 + 2)
                for i in range(NT):
                    rows_layer(4 + i, slice(0, W), zhi, zlo, W_T1, i).then_inc(top1, 1)

            def turn_r(t):
                pe.wait_ge(t1_read, t * 2 + 2)
                pe.wait_ge(z_done, t * 4 + 4)
                turn(tx, 6, r_turned)

            def top_two(t):
                pe.wait_ge(w_split, NP)
                pe.wait_ge(r_split, t + 1)
                for i in range(NT):
                    mm = rows_layer(4, slice(i * TOP2, (i + 1) * TOP2), rhi, rlo, W_T2, i, TOP2)
                mm.then_inc(top2, 1)

            def body(t1, t2):
                if t1 is not None:
                    turn_sup(t1)
                if t2 is not None:
                    post(t2)
                if t1 is not None:
                    measure(t1, 0)
                    measure(t1, 1)
                if t2 is not None:
                    turn_z(t2)
                if t1 is not None:
                    measure(t1, 2)
                if t2 is not None:
                    top_one(t2)
                if t1 is not None:
                    measure(t1, 3)
                if t2 is not None:
                    turn_r(t2)
                    top_two(t2)

            pipeline(pe, body)


def build(nc, g):
    with ExitStack() as ctx:
        g.ps = ctx.enter_context(nc.psum_tensor("banks", [P, 8, W], F32))
        g.cols = ctx.enter_context(nc.sbuf_tensor("cols", [P, NCOL], F32))
        g.ident = ctx.enter_context(nc.sbuf_tensor("ident", [P, P], F32))
        g.mask = ctx.enter_context(nc.sbuf_tensor("mask", [P, N, GB], F32))
        g.eps_ln = ctx.enter_context(nc.sbuf_tensor("eps_ln", [P, 1], F32))
        g.tiny = ctx.enter_context(nc.sbuf_tensor("tiny", [P, 1], F32))
        g.none = ctx.enter_context(nc.sbuf_tensor("none", [P, 1], F32))
        g.tiny_hd = ctx.enter_context(nc.sbuf_tensor("tiny_hd", [P, 1], F32))
        phase_constants(nc, g)
        with nc.sbuf_tensor("stats", [P, CHUNKS_A * TT, 6], F32) as g.stats:
            phase_first_layers(nc, g)
            phase_second_layers(nc, g)
        phase_attention(nc, g)
        phase_interfere(nc, g)
        phase_top(nc, g)


class Tensors:
    pass


def layout(inputs):
    import numpy as np
    a = {k: np.asarray(v) for k, v in inputs.items()}
    e = lambda n: a["L0_rec_" + n]
    out = {}
    out["x_t"] = a["r_x"].T.reshape(KI, P, TOK)
    first = [e(b + "_W1").T.reshape(KI, P, 4, W)[:, :, c] for b in ("er", "ei") for c in range(4)]
    first.append(a["W_top1"][OUT:].reshape(KI, P, W))
    out["w_first"] = np.stack(first)
    out["row1"] = np.concatenate([e("er_b1").reshape(4, W), e("ei_b1").reshape(4, W), a["b_top1"].reshape(1, W)])
    second = [e(b + "_W2").T.reshape(8, 2, P, 2, 2, KD, P).transpose(5, 3, 0, 2, 1, 4, 6).reshape(8, 8, P, W)
              for b in ("er", "ei")]
    out["w_second"] = np.concatenate(second)

    def cols(v):
        return v.reshape(-1, P).T
    by_chunk = {n: e(n).reshape(N, KD, P).transpose(1, 0, 2) for n in ("er_b2", "ei_b2")}
    out["cols_in"] = np.concatenate([cols(by_chunk.get(n, e(n)) if n in by_chunk else e(n)) for n in (
        "er_g1", "er_be1", "ei_g1", "ei_be1", "er_b2", "ei_b2", "bq_r", "bq_i", "bk_r", "bk_i", "bv_r", "bv_i",
        "bo_r", "bo_i", "post_g", "post_be")], axis=1)
    pieces = []
    for n in ("Wq_r", "Wq_i", "Wk_r", "Wk_i", "Wv_r", "Wv_i", "Wo_r", "Wo_i"):
        pieces.append(e(n).T.reshape(KD, P, W))
    for n in range(N):
        for t in ("int_Wr", "int_Wi"):
            pieces.append(e(t)[n].T.reshape(KD, P, W))
    for n in ("meas_Mr", "meas_Mi", "post_W"):
        pieces.append(e(n).T.reshape(KD, P, W))
    pieces.append(a["W_top1"][:OUT].reshape(KD, P, W))
    pieces.append(a["W_top2"].reshape(2, 2, P, TOP2).transpose(0, 2, 1, 3).reshape(2, P, W))
    out["w_pieces"] = np.concatenate(pieces)
    out["row2"] = np.concatenate([e("post_b"), a["b_top2"], a["W_top3"][:, 0]]).reshape(1, 1024)
    out["ids"] = a["ids"]
    for f in range(N):
        out[f"tbl_{f}"] = a[f"tbl_{f}"]
    return {k: np.ascontiguousarray(v) for k, v in out.items()}


def program(nc, arrays):
    def tensor(name):
        v = arrays[name]
        return nc.dram_tensor(name, v.shape, mybir.dt.from_np(v.dtype), kind="ExternalInput").ap()

    g = Tensors()
    g.x_t, g.w_first, g.row1 = tensor("x_t"), tensor("w_first"), tensor("row1")
    g.w_second, g.cols_in = tensor("w_second"), tensor("cols_in")
    g.w_pieces, g.row2, g.ids = tensor("w_pieces"), tensor("row2"), tensor("ids")
    g.tbl_0, g.tbl_1, g.tbl_2, g.tbl_3 = tensor("tbl_0"), tensor("tbl_1"), tensor("tbl_2"), tensor("tbl_3")
    g.out = nc.dram_tensor("out", (TOK, 1), F32, kind="ExternalOutput").ap()
    g.h_scr = nc.dram_tensor("h_scr", (CHUNKS_A, TT, P, W), F32, kind="Internal").ap()
    g.s_scr = nc.dram_tensor("s_scr", (2, 2, TOK // GB, P, KD, N, GB), F32, kind="Internal").ap()
    g.a_scr = nc.dram_tensor("a_scr", (TOK // BT, N, P, 4, KD, BT), F32, kind="Internal").ap()
    g.sup_scr = nc.dram_tensor("sup_scr", (TT, P, 2, D), F32, kind="Internal").ap()
    build(nc, g)
    return g


def kernel(**inputs):
    import concourse.bacc as bacc
    from concourse.bass_utils import run_bass_kernel_spmd

    arrays = layout(inputs)
    nc = bacc.Bacc("TRN2", target_bir_lowering=False, num_devices=1)
    program(nc, arrays)
    r = run_bass_kernel_spmd(nc, [arrays], core_ids=[0])
    return r.results[0]["out"]
```

```python
from contextlib import ExitStack

import concourse.bass as bass
import concourse.mybir as mybir

F32 = mybir.dt.float32
F32R = mybir.dt.float32r
BF16 = mybir.dt.bfloat16
U32 = mybir.dt.uint32
ACT = mybir.ActivationFunctionType
ALU = mybir.AluOpType
AX = mybir.AxisListType

P = 128
TOK = 1024
IN, HID, D, N, OUT = 2048, 2048, 512, 4, 512
H = 8
HD = D // H
TOP1, TOP2 = 512, 256
LN_EPS = 1e-5
TINY = 1e-8
W = 512

TT = TOK // P
BT = 64
GB = P // N
KI = IN // P
KD = D // P
CHUNKS_A = 2 * HID // W + 1
MT = N * D // P
RAW = 4
SPL = 4

COL_B2 = 4 * KI
COL_BC = 4 * KI + 2 * MT
COL_PG = COL_BC + 8 * KD
COL_PBE = COL_PG + KD
COL_BVH = COL_PBE + KD
NCOL = COL_BVH + H
PC_ATT, PC_INT, PC_TOP = 0, 8 * KD, 8 * KD + 2 * N * KD
N_TOP = 2 * KD + KD + KD + KD // 2


def split3(mm, out, ahi, alo, bhi, blo, first, last):
    mm(out, ahi, bhi, start=first, stop=False)
    mm(out, ahi, blo, start=False, stop=False)
    return mm(out, alo, bhi, start=False, stop=last)


class Stage:

    def __init__(self, nc, tag):
        self.nc, self.tag, self.ctx = nc, tag, ExitStack()

    def sb(self, name, shape, dt=F32):
        return self.ctx.enter_context(self.nc.sbuf_tensor(f"{self.tag}_{name}", shape, dt))

    def sem(self, name):
        return self.ctx.enter_context(self.nc.semaphore(f"{self.tag}_{name}"))


def phase_constants(nc, g):
    s = Stage(nc, "c")
    with s.ctx:
        zeroed = s.sem("zeroed")
        made = s.sem("made")
        cols_in = s.sem("cols_in")
        block = s.ctx.enter_context(nc.Block())

        @block.sync
        def _(sp):
            sp.dma_start(g.cols[:, :], g.cols_in).then_inc(cols_in, 16)
            sp.wait_ge(cols_in, 16)

        @block.gpsimd
        def _(pool):
            pool.memset(g.ident[:, :], 0.0).then_inc(zeroed, 1)
            pool.memset(g.mask[:, :, :], 0.0).then_inc(zeroed, 1)
            pool.memset(g.eps_ln[:, :], LN_EPS).then_inc(zeroed, 1)
            pool.memset(g.tiny[:, :], TINY).then_inc(zeroed, 1)
            pool.memset(g.tiny_hd[:, :], TINY / HD).then_inc(zeroed, 1)
            pool.memset(g.none[:, :], 0.0).then_inc(zeroed, 1)
            pool.wait_ge(zeroed, 6)
            pool.affine_select(out=g.ident[:, :], in_=g.ident[:, :], compare_op=ALU.not_equal, fill=1.0, base=0,
                               pattern=[[-1, P]], channel_multiplier=1).then_inc(made, 1)
            for q in range(N):
                pool.wait_ge(made, q + 1)
                pool.affine_select(out=g.mask[:, :, :], in_=g.mask[:, :, :], compare_op=ALU.not_equal, fill=1.0,
                                   base=-GB * q, pattern=[[0, N], [-1, GB]], channel_multiplier=1).then_inc(made, 1)
            pool.wait_ge(made, N + 1)


def phase_first_layers(nc, g):
    s = Stage(nc, "a")
    XRAW = 4
    with s.ctx:
        xraw = s.sb("xraw", [P, XRAW, TOK])
        xhi = s.sb("xhi", [P, KI, TOK], F32R)
        xlo = s.sb("xlo", [P, KI, TOK], F32R)
        wraw = s.sb("wraw", [P, RAW, W])
        whi = s.sb("whi", [P, SPL, W], F32R)
        wlo = s.sb("wlo", [P, SPL, W], F32R)
        bias = s.sb("bias", [P, CHUNKS_A * W])
        hst = s.sb("hst", [P, TT, W])
        x_loaded = [s.sem(f"x_loaded{i}") for i in range(XRAW)]
        x_hi = s.sem("x_hi")
        x_split = s.sem("x_split")
        w_loaded = [s.sem(f"w_loaded{i}") for i in range(RAW)]
        w_hi = s.sem("w_hi")
        w_split = s.sem("w_split")
        w_used = s.sem("w_used")
        bank_full = s.sem("bank_full")
        bank_read = s.sem("bank_read")
        stats_done = s.sem("stats_done")
        bias_in = s.sem("bias_in")
        stored = [s.sem(f"stored{i}") for i in range(TT)]
        block = s.ctx.enter_context(nc.Block())

        @block.sync
        def _(sp):
            sp.dma_start(bias[:, :], g.row1.rearrange("c n -> (c n)").partition_broadcast(P)).then_inc(bias_in, 16)
            with sp.Fori(0, CHUNKS_A) as c:
                for k in range(KI):
                    sp.wait_ge(w_split, c * KI + (k + 1))
                    sp.dma_start(wraw[:, k % RAW, :], g.w_first[c, k]).then_inc(w_loaded[k % RAW], 16)

        @block.gpsimd
        def _(pool):
            for k in range(KI):
                if k >= XRAW:
                    pool.wait_ge(x_split, k - XRAW + 1)
                pool.dma_start(xraw[:, k % XRAW, :], g.x_t[k]).then_inc(x_loaded[k % XRAW], 16)
            with pool.Fori(0, CHUNKS_A) as c:
                for t in range(TT):
                    pool.wait_ge(bank_read, c * TT + (TT + t + 1))
                    pool.dma_start(g.h_scr[c, t], hst[:, t, :]).then_inc(stored[t], 16)
            for t in range(TT):
                pool.wait_ge(stored[t], 16 * CHUNKS_A)
            pool.wait_ge(stats_done, TT * CHUNKS_A)

        @block.scalar
        def _(act):
            def w_high(c, k):
                act.wait_ge(w_loaded[k % RAW], c * (16 * KI // RAW) + 16 * (k // RAW + 1))
                act.wait_ge(w_used, c * KI + (k + 1))
                act.activation(whi[:, k % SPL, :], wraw[:, k % RAW, :], ACT.Copy).then_inc(w_hi, 1)

            for k in range(KI):
                act.wait_ge(x_loaded[k % XRAW], 16 * (k // XRAW + 1))
                act.activation(xhi[:, k, :], xraw[:, k % XRAW, :], ACT.Copy).then_inc(x_hi, 1)
                w_high(0, k)
            with act.Fori(1, CHUNKS_A) as c:
                for k in range(KI):
                    w_high(c, k)

        @block.vector
        def _(dve):
            def w_low(c, k):
                dve.wait_ge(w_hi, c * KI + (k + 1))
                dve.tensor_tensor(wlo[:, k % SPL, :], wraw[:, k % RAW, :], whi[:, k % SPL, :].bitcast(F32),
                                  ALU.subtract).then_inc(w_split, 1)

            def evacuate(c):
                for t in range(TT):
                    dve.wait_ge(bank_full, c * TT + (t + 1))
                    dve.wait_ge(stored[t], c * 16)
                    dve.wait_ge(stats_done, c * TT)
                    dve.tensor_tensor(hst[:, t, :], g.ps[:, t, :], bias[:, bass.ts(c, W)],
                                      ALU.add).then_inc(bank_read, 1)
                for t in range(TT):
                    dve.wait_ge(bank_read, c * TT + (TT + t + 1))
                    dve.bn_stats(g.stats[:, bass.ds(c * TT + t, 1), :], hst[:, t, :]).then_inc(stats_done, 1)

            dve.sem_inc(w_split, RAW)
            for k in range(KI):
                dve.wait_ge(x_hi, k + 1)
                dve.tensor_tensor(xlo[:, k, :], xraw[:, k % XRAW, :], xhi[:, k, :].bitcast(F32),
                                  ALU.subtract).then_inc(x_split, 1)
                w_low(0, k)
            dve.wait_ge(bias_in, 16)
            AHEAD = 3
            for k in range(AHEAD):
                w_low(1, k)
            evacuate(0)
            with dve.Fori(1, CHUNKS_A - 1) as c:
                for k in range(AHEAD, KI):
                    w_low(c, k)
                for k in range(AHEAD):
                    w_low(c + 1, k)
                evacuate(c)
            for k in range(AHEAD, KI):
                w_low(CHUNKS_A - 1, k)
            evacuate(CHUNKS_A - 1)

        @block.tensor
        def _(pe):
            pe.sem_inc(w_used, SPL)
            pe.sem_inc(bank_read, TT)
            with pe.Fori(0, CHUNKS_A) as c:
                for k in range(KI):
                    pe.wait_ge(x_split, k + 1)
                    pe.wait_ge(w_split, c * KI + (RAW + k + 1))
                    for t in range(TT):
                        if k == 0:
                            pe.wait_ge(bank_read, c * TT + (t + 1))
                        m = split3(pe.matmul, g.ps[:, t, :], xhi[:, k, t * P:(t + 1) * P], xlo[:, k, t * P:(t + 1) * P],
                                   whi[:, k % SPL, :], wlo[:, k % SPL, :], k == 0, k == KI - 1)
                        if k == KI - 1 and t < TT - 1:
                            m.then_inc(bank_full, 1)
                    if k < KI - 1:
                        m.then_inc(w_used, 1)
                m.then_inc(bank_full, 1)
                pe.drain().then_inc(w_used, 1)


def phase_second_layers(nc, g):
    s = Stage(nc, "b")
    CH, ST = 8, 8
    HW = 256
    AHEAD = 3
    with s.ctx:
        ghi = s.sb("ghi", [P, KI, TOK], F32R)
        glo = s.sb("glo", [P, KI, TOK], F32R)
        wraw = s.sb("wraw", [P, RAW, W])
        whi = s.sb("whi", [P, SPL, 2, 256], F32R)
        wlo = s.sb("wlo", [P, SPL, 2, 256], F32R)
        hl = s.sb("hl", [P, 2, TT, HW])
        gf = s.sb("gf", [P, 2, TOK])
        shi = s.sb("shi", [P, 2, W // GB, 2, GB], F32R)
        slo = s.sb("slo", [P, 2, W // GB, 2, GB], F32R)
        mv = s.sb("mv", [P, 2 * TT, 2])
        rstd = s.sb("rstd", [P, 2 * TT])
        b2 = s.sb("b2", [P, 2])
        b2_ready = s.sem("b2_ready")
        mv_done = s.sem("mv_done")
        std_done = s.sem("std_done")
        rstd_done = s.sem("rstd_done")
        w_loaded = [s.sem(f"w_loaded{i}") for i in range(RAW)]
        w_hi = s.sem("w_hi")
        w_split = s.sem("w_split")
        w_used = s.sem("w_used")
        h_loaded = [s.sem(f"h_loaded{i}") for i in range(2)]
        h_normed = s.sem("h_normed")
        turned = s.sem("turned")
        gelu_done = s.sem("gelu_done")
        g_hi = s.sem("g_hi")
        g_split = s.sem("g_split")
        acc_full = s.sem("acc_full")
        s_hi = s.sem("s_hi")
        s_split = s.sem("s_split")
        st_hi = [s.sem(f"stored_hi{i}") for i in range(2)]
        st_lo = [s.sem(f"stored_lo{i}") for i in range(2)]
        block = s.ctx.enter_context(nc.Block())
        acc = [g.ps[:, 4 + i, :] for i in range(4)]

        @block.sync
        def _(sp):
            with sp.Fori(0, 2 * CH) as c:
                for j in range(ST):
                    sp.wait_ge(w_split, c * ST + (j + 1))
                    sp.dma_start(wraw[:, j % RAW, :], g.w_second[c, j]).then_inc(w_loaded[j % RAW], 16)

        @block.gpsimd
        def _(pool):
            def load_h(br, j):
                pool.wait_ge(turned, br * KI + (2 * j + 2))
                src = g.h_scr[br * 4 + j // 2, :, :, (j % 2) * HW:(j % 2) * HW + HW]
                pool.dma_start(hl[:, j % 2, :, :], src.rearrange("t p f -> p t f")).then_inc(h_loaded[j % 2], 16)

            load_h(0, 0)
            load_h(0, 1)
            for br in range(2):
                for j in range(2, ST):
                    load_h(br, j)
                if br == 0:
                    load_h(1, 0)
                    load_h(1, 1)
                with pool.Fori(0, KD) as k:
                    for pair in range(2):
                        for half in range(2):
                            for h, t, done, sent in ((0, shi, s_hi, st_hi), (1, slo, s_split, st_lo)):
                                pool.wait_ge(done, br * (4 * CH) + k * 8 + (4 * pair + 2 * half + 2 + 4 * h))
                                dst = g.s_scr.rearrange(
                                        "e h c p k n b -> p e h c k (n b)")[
                                    :, br:br + 1, h, half * (W // GB):(half + 1) * (W // GB), bass.ds(k, 1),
                                    2 * pair * GB:2 * pair * GB + 2 * GB]
                                pool.dma_start(dst.rearrange("p e c k x -> p (e c k) x"),
                                               t[:, half, :, :, :].bitcast(F32).rearrange("p c n b -> p c (n b)")).then_inc(
                                                   sent[half], 16)
            for half in range(2):
                pool.wait_ge(st_hi[half], 16 * 2 * CH)
                pool.wait_ge(st_lo[half], 16 * 2 * CH)

        @block.scalar
        def _(act):
            def w_high(c, j):
                act.wait_ge(w_loaded[j % RAW], c * (16 * ST // RAW) + 16 * (j // RAW + 1))
                act.wait_ge(w_used, c * ST + (j + 1))
                act.activation(whi[:, j % SPL, :, :].rearrange("p a n -> p (a n)"), wraw[:, j % RAW, :],
                               ACT.Copy).then_inc(w_hi, 1)

            def s_high(br, c):
                for b in range(4):
                    cc = br * CH + c
                    act.wait_ge(acc_full, cc * 4 + (b + 1))
                    act.wait_ge(st_hi[b // 2], cc * 16)
                    act.wait_ge(b2_ready, cc + 1)
                    act.activation(shi[:, b // 2, :, b % 2, :], acc[b].rearrange("p (g b) -> p g b", b=GB), ACT.Identity,
                                   bias=b2[:, b % 2:b % 2 + 1]).then_inc(s_hi, 1)

            def gain_shift(br, x, k):
                i = (2 * br + x) * KI + k
                return g.cols[:, i:i + 1]

            act.wait_ge(mv_done, 2 * TT)
            act.activation(rstd[:, :], mv[:, :, 1], ACT.Sqrt, bias=g.eps_ln[:, :]).then_inc(std_done, 1)
            for br in range(2):
                for j in range(ST):
                    w_high(br * CH, j)
                    for k in (2 * j, 2 * j + 1):
                        act.wait_ge(turned, br * KI + (4 + k + 1))
                        act.wait_ge(g_split, br * KI + (k + 1))
                        if k == 0:
                            act.wait_ge(w_used, br * (CH * ST) + SPL)
                        act.activation(gf[:, k % 2, :], g.ps[:, 2 * (k % 2):2 * (k % 2) + 2, :].rearrange("p a n -> p (a n)"),
                                       ACT.Gelu, bias=gain_shift(br, 1, k),
                                       scale=gain_shift(br, 0, k)).then_inc(gelu_done, 1)
                        act.wait_ge(gelu_done, br * KI + (2 + k + 1))
                        act.activation(ghi[:, k, :], gf[:, k % 2, :], ACT.Copy).then_inc(g_hi, 1)
                for j in range(AHEAD):
                    w_high(br * CH + 1, j)
                s_high(br, 0)
                with act.Fori(1, CH - 1) as c:
                    for j in range(AHEAD, ST):
                        w_high(br * CH + c, j)
                    for j in range(AHEAD):
                        w_high(br * CH + c + 1, j)
                    s_high(br, c)
                for j in range(AHEAD, ST):
                    w_high(br * CH + (CH - 1), j)
                s_high(br, CH - 1)

        @block.vector
        def _(dve):
            def w_low(c, j):
                dve.wait_ge(w_hi, c * ST + (j + 1))
                dve.tensor_tensor(wlo[:, j % SPL, :, :].rearrange("p a n -> p (a n)"), wraw[:, j % RAW, :],
                                  whi[:, j % SPL, :, :].bitcast(F32).rearrange("p a n -> p (a n)"),
                                  ALU.subtract).then_inc(w_split, 1)

            def chunk_bias(cc):
                dve.tensor_copy(b2[:, :], g.cols[:, bass.ds(cc * 2 + COL_B2, 2)]).then_inc(b2_ready, 1)

            def s_low(br, c):
                chunk_bias(br * CH + c)
                dve.wait_ge(b2_ready, br * CH + (c + 1))
                for b in range(4):
                    cc = br * CH + c
                    dve.wait_ge(s_hi, cc * 4 + (b + 1))
                    dve.wait_ge(st_lo[b // 2], cc * 16)
                    dve.scalar_tensor_tensor(out=slo[:, b // 2, :, b % 2, :],
                                             in0=acc[b].rearrange("p (g b) -> p g b", b=GB),
                                             scalar=b2[:, b % 2:b % 2 + 1],
                                             in1=shi[:, b // 2, :, b % 2, :].bitcast(F32), op0=ALU.add,
                                             op1=ALU.subtract).then_inc(s_split, 1)

            def normalise(br, j):
                dve.wait_ge(h_loaded[j % 2], br * (16 * ST // 2) + 16 * (j // 2 + 1))
                for t in range(TT):
                    i = br * TT + t
                    m = dve.tensor_scalar(hl[:, j % 2, t, :], hl[:, j % 2, t, :], mv[:, i, 0:1], rstd[:, i:i + 1],
                                          ALU.subtract, ALU.mult)
                m.then_inc(h_normed, 1)

            dve.sem_inc(w_split, RAW)
            dve.sem_inc(g_split, 2)
            dve.sem_inc(s_split, 4)
            for br in range(2):
                for t in range(TT):
                    v = g.stats[:, :, :].rearrange("p (c t) s -> p c t s", t=TT)[:, 4 * br:4 * br + 4, t, :]
                    dve.bn_aggr(mv[:, br * TT + t, :], v).then_inc(mv_done, 1)
            dve.wait_ge(std_done, 1)
            dve.reciprocal(rstd[:, :], rstd[:, :]).then_inc(rstd_done, 1)
            dve.wait_ge(rstd_done, 1)
            for br in range(2):
                if br == 0:
                    normalise(0, 0)
                for j in range(ST):
                    w_low(br * CH, j)
                    if j + 1 < ST:
                        normalise(br, j + 1)
                    for k in (2 * j, 2 * j + 1):
                        dve.wait_ge(g_hi, br * KI + (k + 1))
                        dve.tensor_tensor(glo[:, k, :], gf[:, k % 2, :], ghi[:, k, :].bitcast(F32),
                                          ALU.subtract).then_inc(g_split, 1)
                for j in range(AHEAD):
                    w_low(br * CH + 1, j)
                s_low(br, 0)
                with dve.Fori(1, CH - 1) as c:
                    for j in range(AHEAD, ST):
                        w_low(br * CH + c, j)
                    for j in range(AHEAD):
                        w_low(br * CH + c + 1, j)
                    s_low(br, c)
                if br == 0:
                    normalise(1, 0)
                for j in range(AHEAD, ST):
                    w_low(br * CH + (CH - 1), j)
                s_low(br, CH - 1)

        @block.tensor
        def _(pe):
            def turn(br, k):
                pe.wait_ge(h_normed, br * ST + (k // 2 + 1))
                pe.wait_ge(gelu_done, br * KI + (k + 1))
                for t in range(TT):
                    m = pe.transpose(g.ps[:, 2 * (k % 2) + t // 4, (t % 4) * P:(t % 4 + 1) * P],
                                     hl[:, (k // 2) % 2, t, (k % 2) * P:(k % 2 + 1) * P], g.ident[:, :])
                m.then_inc(turned, 1)

            def multiply(cc, j, br=None):
                pe.wait_ge(w_split, cc * ST + (RAW + j + 1))
                if br is not None:
                    pe.wait_ge(g_split, br * KI + (2 + 2 * j + 2))
                for b in range(4):
                    half, m = b // 2, b % 2
                    if j == 0:
                        pe.wait_ge(s_split, cc * 4 + (b + 1))
                    for i in range(2):
                        k = 2 * j + i
                        cols = slice(half * W, half * W + W)
                        mm = split3(pe.matmul, acc[b], whi[:, j % SPL, i, m * P:(m + 1) * P],
                                    wlo[:, j % SPL, i, m * P:(m + 1) * P], ghi[:, k, cols], glo[:, k, cols],
                                    k == 0, k == KI - 1)
                    if j == ST - 1:
                        mm.then_inc(acc_full, 1)
                if j == ST - 1:
                    pe.drain().then_inc(w_used, 1)
                else:
                    mm.then_inc(w_used, 1)

            pe.sem_inc(w_used, SPL)
            pe.sem_inc(turned, 4)
            pe.sem_inc(gelu_done, 2)
            for br in range(2):
                if br == 0:
                    turn(0, 0)
                    turn(0, 1)
                for j in range(ST):
                    if j + 1 < ST:
                        turn(br, 2 * j + 2)
                        turn(br, 2 * j + 3)
                    multiply(br * CH, j, br)
                with pe.Fori(1, CH - 1) as c:
                    for j in range(ST):
                        multiply(br * CH + c, j)
                if br == 0:
                    turn(1, 0)
                    turn(1, 1)
                for j in range(ST):
                    multiply(br * CH + CH - 1, j)


def phase_attention(nc, g):
    s = Stage(nc, "t")
    NB = TOK // BT
    C = N * BT
    NG = BT // GB
    GH = NG * 2
    NP = 8 * KD
    TR = 6
    M_Q, M_K, M_V, M_O = 0, 2, 4, 6
    with s.ctx:
        wraw = s.sb("wraw", [P, 2, W])
        whi = s.sb("whi", [P, NP, W], F32R)
        wlo = s.sb("wlo", [P, NP, W], F32R)
        sx = s.sb("sx", [P, 2, 2, NG, KD, P], F32R)
        qs = s.sb("qs", [P, 2, 2, C])
        ks = s.sb("ks", [P, 2, 2, 2, C])
        v = s.sb("v", [P, NG, H, 2, HD])
        sq = s.sb("sq", [P, 2, W])
        m2 = s.sb("m2", [P, W])
        pd = s.sb("pd", [P, GH, N, GB])
        ptl = s.sb("ptl", [P, 2, W])
        sc = s.sb("sc", [P, 7, GH, N])
        ohi = s.sb("ohi", [P, KD, 2, C], F32R)
        olo = s.sb("olo", [P, KD, 2, C], F32R)
        at = s.sb("at", [P, 2, 2, 2, C], F32R)
        ahi, alo = at[:, 0], at[:, 1]
        w_loaded = [s.sem(f"w_loaded{i}") for i in range(TR)]
        w_hi = s.sem("w_hi")
        w_split = s.sem("w_split")
        s_loaded = [s.sem(f"s_loaded{e}") for e in range(2)]
        projected = s.sem("projected")
        q_read = s.sem("q_read")
        k_read = s.sem("k_read")
        v_full = s.sem("v_full")
        v_read = s.sem("v_read")
        scored = s.sem("scored")
        squared = s.sem("squared")
        step = s.sem("step")
        mag_done = s.sem("mag_done")
        exp_done = s.sem("exp_done")
        p_turned = s.sem("p_turned")
        pt_read = s.sem("pt_read")
        mixed = s.sem("mixed")
        o_hi = s.sem("o_hi")
        o_split = s.sem("o_split")
        wo_full = s.sem("wo_full")
        a_hi = s.sem("a_hi")
        a_split = s.sem("a_split")
        stored = [s.sem(f"stored{i}") for i in range(2)]
        block = s.ctx.enter_context(nc.Block())
        b_qk, b_sc, b_pt, b_mx = (g.ps[:, 2 * i:2 * i + 2, :] for i in range(4))

        def raw(i):
            i %= TR
            if i < 2:
                return wraw[:, i, :]
            return at[:, (i - 2) // 2, (i - 2) % 2].rearrange("p e c -> p (e c)").bitcast(F32)

        def half(h):
            return slice(h * HD, (h + 1) * HD)

        def bcol(mat, m, rows=slice(0, P)):
            return g.cols[rows, COL_BC + mat * KD + m:COL_BC + mat * KD + m + 1]

        def by_group(ap):
            return ap.rearrange("p (g n b) -> p g n b", g=NG, n=N)

        def by_state(ap):
            return ap.rearrange("p (n g b) -> p g n b", g=NG, n=N)

        def blocks(eng, body):
            body(0, True, False)
            with eng.Fori(1, NB - 1) as b:
                body(b, False, False)
            body(NB - 1, False, True)

        @block.sync
        def _(sp):
            def load_s(b):
                for e in range(2):
                    for h in range(2):
                        src = g.s_scr[e, h].rearrange("c p k n b -> p c (k n b)")[:, bass.ds(b * NG, NG), :]
                        sp.dma_start(sx[:, e, h, :, :, :].bitcast(F32).rearrange("p g k c -> p g (k c)"),
                                     src).then_inc(s_loaded[e], 16)

            def store(b):
                for m in range(KD):
                    sp.wait_ge(a_split, b * 8 + (2 * m + 2))
                    for e in range(2):
                        for h, t in enumerate((ahi, alo)):
                            dst = g.a_scr.rearrange("b n p v k t -> b v k p n t")[bass.ds(b, 1), 2 * e + h, m]
                            sp.dma_start(dst.rearrange("o p n t -> p (o n) t"), t[:, m % 2, e, :].bitcast(F32).rearrange(
                                "p (n t) -> p n t", n=N)).then_inc(stored[m % 2], 16)

            def body(b, first, last):
                if not first:
                    store(b - 1)
                if not last:
                    sp.wait_ge(projected, b * 8 + 8)
                    sp.wait_ge(v_full, b * 4 + 4)
                    load_s(b + 1)

            for i in range(2):
                sp.sem_inc(stored[i], 64)
            load_s(0)
            for i in range(NP):
                if i >= TR:
                    sp.wait_ge(w_split, i - TR + 1)
                sp.dma_start(raw(i), g.w_pieces[PC_ATT + i]).then_inc(w_loaded[i % TR], 16)
            blocks(sp, body)
            store(NB - 1)
            for i in range(2):
                sp.wait_ge(stored[i], 64 * (2 * NB + 1))

        @block.scalar
        def _(act):
            def q_evac(b, m):
                act.wait_ge(projected, b * 8 + (2 * m + 1))
                if not isinstance(b, int) or 4 * b + m >= 2:
                    act.wait_ge(scored, b * 8 + (2 * m - 2))
                for e in range(2):
                    for h in range(2):
                        ins = act.activation(qs[half(e), m % 2, h, :], b_qk[half(h), 0, e * C:(e + 1) * C], ACT.Identity,
                                             bias=bcol(M_Q + e, m, half(h)))
                    ins.then_inc(q_read, 1)

            def square(b, m, h):
                act.wait_ge(scored, b * 8 + (2 * m + h + 1))
                act.wait_ge(step, b * 32 + 8 * m)
                act.activation(sq[:, h, :], b_sc[:, h, :], ACT.Square).then_inc(squared, 1)

            def pt_evac(b, m):
                act.wait_ge(p_turned, b * 4 + (m + 1))
                if not isinstance(b, int) or 4 * b + m >= 2:
                    act.wait_ge(mixed, b * 4 + (m - 1))
                act.activation(ptl[:, m % 2, :], b_pt[:, m % 2, :], ACT.Copy).then_inc(pt_read, 1)

            def o_high(b, m):
                act.wait_ge(mixed, b * 4 + (m + 1))
                for e in range(2):
                    for h in range(2):
                        x = COL_BVH + 2 * m + h
                        ins = act.activation(ohi[half(h), m, e, :], b_mx[half(e), m % 2, h * C:(h + 1) * C], ACT.Identity,
                                             bias=g.cols[half(e), x:x + 1])
                    ins.then_inc(o_hi, 1)

            def a_high(b, m):
                act.wait_ge(wo_full, b * 4 + (m + 1))
                act.wait_ge(stored[m % 2], b * 128 + 64 * (m // 2 + 1))
                for e in range(2):
                    act.activation(by_state(ahi[:, m % 2, e, :]), by_group(b_qk[:, m % 2, e * C:(e + 1) * C]), ACT.Identity,
                                   bias=bcol(M_O + e, m)).then_inc(a_hi, 1)

            def before(b, m):
                return (b, m - 1) if m else (b - 1, KD - 1)

            def body(b, first, last):
                for m in range(KD):
                    if m < KD - 1:
                        q_evac(b, m + 1)
                        if not (first and m == 0):
                            pt_evac(*before(b, m))
                    if first and m == 0:
                        pieces(M_V * KD, M_O * KD)
                    if first and m == 2:
                        pieces(M_O * KD, NP)
                    square(b, m, 0)
                    square(b, m, 1)
                    if m == KD - 1:
                        if last:
                            pt_evac(b, m - 1)
                        else:
                            q_evac(b + 1, 0)
                            pt_evac(b, m - 1)
                    act.wait_ge(step, b * 32 + (8 * m + 3))
                    act.activation(sc[:, 1, :, :], sc[:, 0, :, :], ACT.Sqrt, scale=1.0 / HD,
                                   bias=g.tiny_hd[:, :]).then_inc(mag_done, 1)
                    act.wait_ge(step, b * 32 + (8 * m + 5))
                    act.activation(sc[:, 4, :, :], sc[:, 3, :, :], ACT.Exp).then_inc(exp_done, 1)
                    if not (first and m == 0):
                        o_high(*before(b, m))
                    if m == 0:
                        for i in range(2 * NG):
                            act.wait_ge(v_full, b * 4 + (i + 1))
                            act.activation(v[:, i // 2, :, i % 2, :],
                                           b_qk[:, i % 2, :].rearrange("p (h d) -> p h d", h=H),
                                           ACT.Copy).then_inc(v_read, 1)
                        if not first:
                            for mm in range(KD):
                                a_high(b - 1, mm)

            def pieces(i0, i1):
                for i in range(i0, i1):
                    act.wait_ge(w_loaded[i % TR], 16 * (i // TR + 1))
                    act.activation(whi[:, i, :], raw(i), ACT.Copy).then_inc(w_hi, 1)

            pieces(0, M_V * KD)
            q_evac(0, 0)
            blocks(act, body)
            pt_evac(NB - 1, KD - 1)
            o_high(NB - 1, KD - 1)
            for m in range(KD):
                a_high(NB - 1, m)

        @block.vector
        def _(dve):
            def k_evac(b, m):
                dve.wait_ge(projected, b * 8 + (2 * m + 2))
                if not isinstance(b, int) or 4 * b + m >= 2:
                    dve.wait_ge(scored, b * 8 + (2 * m - 2))
                for e, part, at_half, sign in ((0, 0, 0, 1), (0, 1, 1, 1), (1, 0, 1, 1), (1, 1, 0, -1)):
                    for h in range(2):
                        ins = dve.tensor_scalar(ks[half(at_half), m % 2, h, part, :], b_qk[half(h), 1, e * C:(e + 1) * C],
                                                bcol(M_K + e, m, half(h)), float(sign), ALU.add, ALU.mult)
                    ins.then_inc(k_read, 1)

            def softmax(b, m, unit=None):
                done = [0]

                def link(ins):
                    ins.then_inc(step, 1)
                    done[0] += 1
                    dve.wait_ge(step, b * 32 + (8 * m + done[0]))

                dve.wait_ge(squared, b * 8 + (2 * m + 2))
                sqv = sq[:, :, :].rearrange("p h (a c) -> p a h c", a=2)
                link(dve.tensor_tensor(m2[:, :].rearrange("p (h c) -> p h c", h=2), sqv[:, 0], sqv[:, 1], ALU.add))
                sqv = m2[:, :].rearrange("p (g c) -> p g c", g=GH)
                mask = g.mask[:, :, :].rearrange("p n b -> p (n b)").unsqueeze(1).to_broadcast([P, GH, P])
                link(dve.tensor_tensor(sqv, sqv, mask, ALU.mult))
                link(dve.tensor_reduce(sc[:, 0, :, :].rearrange("p g n -> p (g n)"),
                                       m2[:, :].rearrange("p (x b) -> p x b", b=GB), AX.X, ALU.add))
                if unit is not None:
                    k_evac(*unit)
                dve.wait_ge(mag_done, b * 4 + (m + 1))
                link(dve.tensor_reduce(sc[:, 2, :, 0], sc[:, 1, :, :], AX.X, ALU.max))
                link(dve.tensor_tensor(sc[:, 3, :, :], sc[:, 1, :, :],
                                       sc[:, 2, :, 0:1].to_broadcast([P, GH, N]), ALU.subtract))
                dve.wait_ge(exp_done, b * 4 + (m + 1))
                link(dve.tensor_reduce(sc[:, 2, :, 1], sc[:, 4, :, :], AX.X, ALU.add))
                link(dve.reciprocal(sc[:, 2, :, 2], sc[:, 2, :, 1]))
                for x in range(GH):
                    dve.wait_ge(p_turned, b * 4 + m) if x == 0 else None
                    ins = dve.scalar_tensor_tensor(
                        out=pd[:, x, :, :], in0=sc[:, 4, x, :].unsqueeze(2).to_broadcast([P, N, GB]),
                        scalar=sc[:, 2, x, 2:3], in1=g.mask[:, :, :], op0=ALU.mult, op1=ALU.mult)
                ins.then_inc(step, 1)

            def o_low(b, m):
                dve.wait_ge(o_hi, b * 8 + (2 * m + 2))
                for e in range(2):
                    for h in range(2):
                        ins = dve.scalar_tensor_tensor(
                            out=olo[half(h), m, e, :], in0=b_mx[half(e), m % 2, h * C:(h + 1) * C],
                            scalar=bcol(M_V + e, m, half(h)), in1=ohi[half(h), m, e, :].bitcast(F32),
                            op0=ALU.add, op1=ALU.subtract)
                    ins.then_inc(o_split, 1)

            def a_low(b, m):
                dve.wait_ge(stored[m % 2], b * 128 + 64 * (m // 2 + 1))
                dve.wait_ge(a_hi, b * 8 + (2 * m + 2))
                for e in range(2):
                    for gr in range(NG):
                        ins = dve.scalar_tensor_tensor(
                            out=by_state(alo[:, m % 2, e, :])[:, gr], in0=by_group(b_qk[:, m % 2, e * C:(e + 1) * C])[:, gr],
                            scalar=bcol(M_O + e, m), in1=by_state(ahi[:, m % 2, e, :].bitcast(F32))[:, gr],
                            op0=ALU.add, op1=ALU.subtract)
                    ins.then_inc(a_split, 1)

            def before(b, m):
                return (b, m - 1) if m else (b - 1, KD - 1)

            def body(b, first, last):
                for m in range(KD):
                    if m < KD - 1:
                        k_evac(b, m + 1)
                    if first and m == 0:
                        pieces(M_V * KD, M_O * KD)
                    if first and m == 2:
                        pieces(M_O * KD, NP)
                    softmax(b, m, (b + 1, 0) if m == KD - 1 and not last else None)
                    if not (first and m == 0):
                        o_low(*before(b, m))
                    if m == 0 and not first:
                        for mm in range(KD):
                            a_low(b - 1, mm)

            def pieces(i0, i1):
                for i in range(i0, i1):
                    dve.wait_ge(w_hi, i + 1)
                    dve.tensor_tensor(wlo[:, i, :], raw(i), whi[:, i, :].bitcast(F32),
                                      ALU.subtract).then_inc(w_split, 1)

            pieces(0, M_V * KD)
            k_evac(0, 0)
            blocks(dve, body)
            o_low(NB - 1, KD - 1)
            for m in range(KD):
                a_low(NB - 1, m)

        @block.tensor
        def _(pe):
            def project(b, m, parts=(0, 1)):
                for i in parts:
                    pe.wait_ge(w_split, (M_Q, M_K)[i] * KD + 2 * KD)
                    pe.wait_ge((q_read, k_read)[i], (b * 4 + m) * (2, 4)[i])
                    if m == 2:
                        pe.wait_ge(v_read, b * 4 + 4)
                        if not (isinstance(b, int) and b == 0):
                            pe.wait_ge(a_split, b * 8 - 2 + 2 * i)
                    for e in range(2):
                        pe.wait_ge(s_loaded[e], b * 32 + 32)
                        for k in range(KD):
                            w = ((M_Q, M_K)[i] + e) * KD + k
                            mm = split3(pe.matmul, b_qk[:, i, e * C:(e + 1) * C], whi[:, w, m * P:(m + 1) * P],
                                        wlo[:, w, m * P:(m + 1) * P], sx[:, e, 0, :, k, :], sx[:, e, 1, :, k, :],
                                        k == 0, k == KD - 1)
                    mm.then_inc(projected, 1)

            def values(b):
                pe.wait_ge(w_split, M_O * KD)
                for i in range(2 * NG):
                    gr, e = i // 2, i % 2
                    if i < 2:
                        pe.wait_ge((q_read, k_read)[i], (b * 4 + 2) * (2, 4)[i])
                    else:
                        pe.wait_ge(v_read, b * 4 + (i - 1))
                    for k in range(KD):
                        w = (M_V + e) * KD + k
                        mm = split3(pe.matmul, b_qk[:, i % 2, :], sx[:, e, 0, gr, k, :], sx[:, e, 1, gr, k, :],
                                    whi[:, w, :], wlo[:, w, :], k == 0, k == KD - 1)
                    mm.then_inc(v_full, 1)

            def score(b, m, h):
                if h == 0:
                    pe.wait_ge(q_read, b * 8 + (2 * m + 2))
                    pe.wait_ge(k_read, b * 16 + (4 * m + 4))
                if not (isinstance(b, int) and b == 0 and m == 0):
                    pe.wait_ge(squared, b * 8 + (2 * m - 1 + h))
                for gr in range(NG):
                    cols = slice(gr * P, (gr + 1) * P)
                    out = b_sc[:, h, :].rearrange("p (a g c) -> p a g c", a=2, g=NG)[:, :, gr]
                    mm = pe.matmul(out, qs[:, m % 2, h, cols], ks[:, m % 2, h, :, cols], start=True, stop=True)
                mm.then_inc(scored, 1)

            def turn(b, m):
                pe.wait_ge(step, b * 32 + (8 * m + 8))
                for x in range(GH):
                    mm = pe.transpose(b_pt[:, m % 2, x * P:(x + 1) * P],
                                      pd[:, x, :, :].rearrange("p n b -> p (n b)"), g.ident[:, :])
                mm.then_inc(p_turned, 1)

            def mix(b, m):
                pe.wait_ge(pt_read, b * 4 + (m + 1))
                pe.wait_ge(v_read, b * 4 + 4)
                if not isinstance(b, int) or 4 * b + m >= 2:
                    pe.wait_ge(o_split, b * 8 + (2 * m - 2))
                for h in range(2):
                    for gr in range(NG):
                        x = h * NG + gr
                        mm = pe.matmul(b_mx[:, m % 2, x * P:(x + 1) * P],
                                       v[:, gr, 2 * m + h, :, :].rearrange("p e d -> p (e d)"),
                                       ptl[:, m % 2, x * P:(x + 1) * P], start=True, stop=True)
                mm.then_inc(mixed, 1)

            def project_out(b, alone=False):
                pe.wait_ge(w_split, NP)
                pe.wait_ge(o_split, b * 8 + 8)
                for m in range(KD):
                    if m < 2 and alone:
                        pe.wait_ge((q_read, k_read)[m], NB * 4 * (2, 4)[m])
                    elif m < 2:
                        pe.wait_ge(v_read, b * 4 + (4 + 3 + m))
                    else:
                        pe.wait_ge(a_split, b * 8 + (2 * m - 2))
                    for e in range(2):
                        for k in range(KD):
                            w = (M_O + e) * KD + k
                            mm = split3(pe.matmul, b_qk[:, m % 2, e * C:(e + 1) * C], whi[:, w, m * P:(m + 1) * P],
                                        wlo[:, w, m * P:(m + 1) * P], ohi[:, k, e, :], olo[:, k, e, :],
                                        k == 0, k == KD - 1)
                    mm.then_inc(wo_full, 1)

            def before(b, m):
                return (b, m - 1) if m else (b - 1, KD - 1)

            def body(b, first, last):
                for m in range(KD - 1):
                    project(b, m + 1)
                    score(b, m, 0)
                    if not (first and m == 0):
                        turn(*before(b, m))
                    score(b, m, 1)
                    if not (first and m == 0):
                        mix(*before(b, m))
                    if m == 0:
                        values(b)
                        if not first:
                            project_out(b - 1)
                score(b, KD - 1, 0)
                score(b, KD - 1, 1)
                if not last:
                    project(b + 1, 0, (0,))
                turn(b, KD - 2)
                if not last:
                    project(b + 1, 0, (1,))
                mix(b, KD - 2)

            project(0, 0)
            blocks(pe, body)
            turn(NB - 1, KD - 1)
            mix(NB - 1, KD - 1)
            project_out(NB - 1, True)


def phase_interfere(nc, g):
    s = Stage(nc, "i")
    NP = 2 * N * KD
    TR = 2 * N
    LEAST = 1e-34
    FLOOR = 2e-38
    HELPED = [(0, 1), (0, 2), (1, 2)]
    STEPS = N + 1 + 3 * 2 + 3 * 4 + 1
    with s.ctx:
        whi = s.sb("whi", [P, NP, W], F32R)
        wlo = s.sb("wlo", [P, NP, W], F32R)
        ax = s.sb("ax", [P, 2, 4, KD, P], F32R)
        ng = s.sb("ng", [P, 2, 2, KD, P], F32R)
        sqi = s.sb("sqi", [P, 2, W])
        mag = s.sb("mag", [P, N, W])
        inv = s.sb("inv", [P, N, W])
        cs = s.sb("cs", [P, 2, N, W])
        zero = s.sb("zero", [P, N, W], BF16)
        zz = s.sb("zz", [P, W], BF16)
        t1 = s.sb("t1", [P, W])
        t2 = s.sb("t2", [P, W])
        pc = s.sb("pc", [P, 2, W])
        sup = s.sb("sup", [P, 2, W])
        ids = s.sb("ids", [P, TT, N], mybir.dt.int32)
        emb = s.sb("emb", [P, TT, N * N])
        st = s.sb("st", [P, N * N])
        nrm = s.sb("nrm", [P, 3])
        k01 = s.sb("k01", [P, 2])
        w_loaded = [s.sem(f"w_loaded{i}") for i in range(TR)]
        w_hi = s.sem("w_hi")
        w_split = s.sem("w_split")
        ids_in = s.sem("ids_in")
        emb_in = s.sem("emb_in")
        k_made = s.sem("k_made")
        a_loaded = [s.sem(f"a_loaded{i}") for i in range(2)]
        a_used = s.sem("a_used")
        negated = s.sem("negated")
        multiplied = s.sem("multiplied")
        squared = s.sem("squared")
        summed = s.sem("summed")
        mag_done = s.sem("mag_done")
        unit = s.sem("unit")
        helped = s.sem("helped")
        taken = s.sem("taken")
        chain = s.sem("chain")
        weighed = s.sem("weighed")
        folded = s.sem("folded")
        len_done = s.sem("len_done")
        len_inv = s.sem("len_inv")
        scaled = s.sem("scaled")
        stored = s.sem("stored")
        block = s.ctx.enter_context(nc.Block())
        raw = cs.rearrange("p a n w -> p (a n) w")

        @block.sync
        def _(sp):
            def load(t, n):
                sp.wait_ge(a_used, t * N + (n + 1))
                for half in range(P // BT):
                    src = g.a_scr[bass.ds(t * (P // BT) + half, 1), n].rearrange("o p v k t -> p (o v k) t")
                    sp.dma_start(ax[:, n % 2, :, :, half * BT:(half + 1) * BT].bitcast(F32).rearrange(
                        "p v k t -> p (v k) t"), src).then_inc(a_loaded[n % 2], 16)

            def store(t):
                sp.wait_ge(scaled, t + 1)
                sp.dma_start(g.sup_scr[bass.ds(t, 1)].rearrange("o p a n -> p (o a n)"),
                             sup[:, :, :].rearrange("p a n -> p (a n)")).then_inc(stored, 16)

            sp.dma_start(ids[:, :, :], g.ids.rearrange("(t p) f -> p t f", p=P)).then_inc(ids_in, 16)
            load(0, 0)
            for i in range(NP):
                if i >= TR:
                    sp.wait_ge(w_split, i - TR + 1)
                sp.dma_start(raw[:, i % TR, :], g.w_pieces[PC_INT + i]).then_inc(w_loaded[i % TR], 16)
                if i == 2 * KD:
                    load(0, 1)
            load(0, 2)
            load(0, 3)
            for n in range(N):
                load(1, n)
            with sp.Fori(2, TT) as t:
                for n in range(N):
                    load(t, n)
                store(t - 2)
            store(TT - 2)
            store(TT - 1)
            sp.wait_ge(stored, 16 * TT)

        @block.gpsimd
        def _(pool):
            def add_squares(t, n):
                pool.wait_ge(squared, t * 8 + (2 * n + 2))
                pool.tensor_tensor(mag[:, n, :], mag[:, n, :], sqi[:, n % 2, :], ALU.add).then_inc(summed, 1)

            def fold(t, i):
                if i == 0:
                    pool.wait_ge(weighed, t * 2 + 2)
                    pool.tensor_tensor(cs[:, :, 2:4, :], cs[:, :, 0:2, :], cs[:, :, 2:4, :], ALU.add).then_inc(folded, 1)
                else:
                    pool.wait_ge(folded, t * 2 + 1)
                    pool.wait_ge(stored, t * 16)
                    pool.tensor_tensor(sup[:, :, :], cs[:, :, 2, :], cs[:, :, 3, :], ALU.add).then_inc(folded, 1)

            def cosine(t, x):
                i, j = HELPED[x]
                pool.wait_ge(unit, t * 8 + (2 * N + 2 * j + 2))
                pool.wait_ge(taken, t * 3 + x)
                for part in range(2):
                    pool.tensor_tensor(pc[:, part, :], cs[:, part, i, :], cs[:, part, j, :], ALU.mult).then_inc(helped, 1)
                pool.wait_ge(helped, t * 9 + (3 * x + 2))
                pool.tensor_tensor(pc[:, 0, :], pc[:, 0, :], pc[:, 1, :], ALU.add).then_inc(helped, 1)

            def body(t, first):
                add_squares(t, 0)
                add_squares(t, 1)
                if not first:
                    fold(t - 1, 0)
                add_squares(t, 2)
                if not first:
                    fold(t - 1, 1)
                cosine(t, 0)
                add_squares(t, 3)
                cosine(t, 1)
                cosine(t, 2)

            pool.memset(k01[:, 0:1], FLOOR).then_inc(k_made, 1)
            pool.memset(k01[:, 1:2], 1.0).then_inc(k_made, 1)
            pool.wait_ge(ids_in, 16)
            for t in range(TT):
                for f, tbl in enumerate((g.tbl_0, g.tbl_1, g.tbl_2, g.tbl_3)):
                    pool.indirect_dma_start(
                        out=emb[:, t, f * N:(f + 1) * N], out_offset=None, in_=tbl,
                        in_offset=bass.IndirectOffsetOnAxis(ap=ids[:, t, f:f + 1].bitcast(U32), axis=0)).then_inc(emb_in, 16)
            body(0, True)
            body(1, False)
            with pool.Fori(2, TT) as t:
                body(t, False)
            fold(TT - 1, 0)
            fold(TT - 1, 1)

        @block.scalar
        def _(act):
            def negate(t, n):
                act.wait_ge(a_loaded[n % 2], t * 64 + (n // 2) * 32 + 32)
                act.wait_ge(a_used, t * N + (n + 1))
                for h in range(2):
                    act.activation(ng[:, n % 2, h, :, :], ax[:, n % 2, 2 + h, :, :].bitcast(F32), ACT.Copy,
                                   scale=-1.0).then_inc(negated, 1)

            def squares(t, n):
                act.wait_ge(multiplied, t * 8 + (2 * n + 2))
                if not (isinstance(t, int) and t == 0):
                    act.wait_ge(chain, t * STEPS)
                act.activation(mag[:, n, :], g.ps[:, n, :], ACT.Square).then_inc(squared, 1)
                if not isinstance(t, int) or 4 * t + n >= 2:
                    act.wait_ge(summed, t * N + (n - 1))
                act.activation(sqi[:, n % 2, :], g.ps[:, N + n, :], ACT.Square).then_inc(squared, 1)

            def magnitude(t, n):
                act.wait_ge(summed, t * N + (n + 1))
                act.activation(zero[:, n, :], mag[:, n, :], ACT.Relu, scale=-1.0 / LEAST, bias=k01[:, 1:2])
                act.activation(mag[:, n, :], mag[:, n, :], ACT.Sqrt, bias=k01[:, 0:1]).then_inc(mag_done, 1)

            def length(t):
                act.wait_ge(folded, t * 2 + 2)
                act.activation(sqi[:, :, :], sup[:, :, :], ACT.Square, accum_out=nrm[:, 0:1]).then_inc(len_done, 1)
                act.wait_ge(len_done, t * 2 + 1)
                act.activation(nrm[:, 1:2], nrm[:, 0:1], ACT.Sqrt, bias=g.tiny[:, :]).then_inc(len_done, 1)

            def scale(t):
                act.wait_ge(len_inv, t + 1)
                act.activation(sup[:, :, :], sup[:, :, :], ACT.Copy, scale=nrm[:, 2:3]).then_inc(scaled, 1)

            negate(0, 0)
            for i in range(NP):
                act.wait_ge(w_loaded[i % TR], 16 * (i // TR + 1))
                act.activation(whi[:, i, :], raw[:, i % TR, :], ACT.Copy).then_inc(w_hi, 1)
                if i == 3 * KD:
                    negate(0, 1)
            act.wait_ge(k_made, 2)

            def body(t, first, last=False):
                squares(t, 0)
                if first:
                    negate(t, 2)
                magnitude(t, 0)
                squares(t, 1)
                if first:
                    negate(t, 3)
                magnitude(t, 1)
                squares(t, 2)
                magnitude(t, 2)
                if not last:
                    negate(t + 1, 0)
                squares(t, 3)
                magnitude(t, 3)
                if not last:
                    negate(t + 1, 1)
                if not first:
                    length(t - 1)
                    scale(t - 1)
                if not last:
                    negate(t + 1, 2)
                    negate(t + 1, 3)

            body(0, True)
            with act.Fori(1, TT - 1) as t:
                body(t, False)
            body(TT - 1, False, True)
            length(TT - 1)
            scale(TT - 1)

        @block.vector
        def _(dve):
            for i in range(NP):
                dve.wait_ge(w_hi, i + 1)
                dve.tensor_tensor(wlo[:, i, :], raw[:, i % TR, :], whi[:, i, :].bitcast(F32),
                                  ALU.subtract).then_inc(w_split, 1)
            dve.wait_ge(emb_in, 16 * TT * N)
            w = inv

            def inverse_length(b):
                dve.wait_ge(len_done, b * 2 + 2)
                dve.reciprocal(nrm[:, 2:3], nrm[:, 1:2]).then_inc(len_inv, 1)

            def body(t, first):
                done = [0]

                def link(ins):
                    ins.then_inc(chain, 1)
                    done[0] += 1
                    dve.wait_ge(chain, t * STEPS + done[0])

                def invert(n):
                    dve.wait_ge(mag_done, t * N + (n + 1))
                    if not first and n == 0:
                        dve.wait_ge(weighed, t * 2)
                    link(dve.reciprocal(inv[:, n, :], mag[:, n, :]))

                def unit_vector(n):
                    if not first and n == 0:
                        dve.wait_ge(folded, (t - 1) * 2 + 1)
                    if not first and n == 2:
                        dve.wait_ge(folded, (t - 1) * 2 + 2)
                    for part in range(2):
                        dve.tensor_tensor(cs[:, part, n, :], g.ps[:, part * N + n, :], inv[:, n, :], ALU.mult).then_inc(unit, 1)

                seen = set()

                def pair(i, j):
                    mark = dve.tensor_tensor(zz[:, :], zero[:, i, :], zero[:, j, :], ALU.add)
                    if (i, j) in HELPED:
                        link(mark)
                        dve.wait_ge(helped, t * 9 + 3 * (HELPED.index((i, j)) + 1))
                        dve.tensor_tensor(t1[:, :], pc[:, 0, :], zz[:, :], ALU.add).then_inc(taken, 1)
                        dve.wait_ge(taken, t * 3 + (HELPED.index((i, j)) + 1))
                    else:
                        dve.tensor_tensor(t1[:, :], cs[:, 0, i, :], cs[:, 0, j, :], ALU.mult)
                        link(dve.tensor_tensor(t2[:, :], cs[:, 1, i, :], cs[:, 1, j, :], ALU.mult))
                        link(dve.tensor_tensor(t1[:, :], t1[:, :], t2[:, :], ALU.add))
                        link(dve.tensor_tensor(t1[:, :], t1[:, :], zz[:, :], ALU.add))
                    for a, b in ((i, j), (j, i)):
                        e = st[:, a * N + b:a * N + b + 1]
                        if b in seen:
                            ins = dve.scalar_tensor_tensor(out=w[:, b, :], in0=t1[:, :], scalar=e, in1=w[:, b, :],
                                                           op0=ALU.mult, op1=ALU.add)
                        else:
                            ins = dve.tensor_scalar(w[:, b, :], t1[:, :], e, st[:, b * N + b:b * N + b + 1],
                                                    ALU.mult, ALU.add)
                            seen.add(b)
                    link(ins)

                invert(0)
                invert(1)
                unit_vector(0)
                unit_vector(1)
                invert(2)
                unit_vector(2)
                link(dve.tensor_copy(st[:, :], emb[:, bass.ds(t, 1), :].rearrange("p o x -> p (o x)")))
                dve.wait_ge(unit, t * 8 + 12)
                pair(0, 1)
                invert(3)
                unit_vector(3)
                dve.wait_ge(unit, t * 8 + 16)
                pair(0, 2)
                pair(0, 3)
                pair(1, 2)
                if not first:
                    inverse_length(t - 1)
                pair(1, 3)
                pair(2, 3)
                link(dve.tensor_tensor(w[:, :, :], w[:, :, :], mag[:, :, :], ALU.mult))
                for part in range(2):
                    dve.tensor_tensor(cs[:, part, :, :], cs[:, part, :, :], w[:, :, :], ALU.mult).then_inc(weighed, 1)
                assert done[0] == STEPS

            body(0, True)
            body(1, False)
            with dve.Fori(2, TT) as t:
                body(t, False)
            inverse_length(TT - 1)

        @block.tensor
        def _(pe):
            pe.sem_inc(a_used, 2)
            pe.sem_inc(unit, 2 * N)
            with pe.Fori(0, TT) as t:
                for n in range(N):
                    pe.wait_ge(w_split, (n + 1) * 2 * KD)
                    pe.wait_ge(a_loaded[n % 2], t * 64 + (n // 2) * 32 + 32)
                    pe.wait_ge(unit, t * 8 + (2 * n + 2))
                    for part in range(2):
                        if part == 0:
                            pe.wait_ge(negated, t * 8 + (2 * n + 2))
                        for x in range(2):
                            for k in range(KD):
                                w = (2 * n + (x if part == 0 else 1 - x)) * KD + k
                                a = ax[:, n % 2, :, k, :]
                                hi, lo = ((a[:, 0], a[:, 1]), (ng[:, n % 2, 0, k, :], ng[:, n % 2, 1, k, :]) if part == 0
                                          else (a[:, 2], a[:, 3]))[x]
                                mm = split3(pe.matmul, g.ps[:, part * N + n, :], hi, lo, whi[:, w, :], wlo[:, w, :],
                                            x == 0 and k == 0, x == 1 and k == KD - 1)
                        mm.then_inc(multiplied, 1)
                    pe.drain().then_inc(a_used, 1)


def phase_top(nc, g):
    s = Stage(nc, "e")
    R = 256
    NB, NT = TOK // R, R // P
    NP, TR = N_TOP, 8
    W_MR, W_MI, W_POST, W_T1, W_T2 = 0, KD, 2 * KD, 3 * KD, 4 * KD
    with s.ctx:
        wraw = s.sb("wraw", [P, TR, W])
        whi = s.sb("whi", [P, NP, W], F32R)
        wlo = s.sb("wlo", [P, NP, W], F32R)
        row = s.sb("row", [P, 2 * W])
        sup = s.sb("sup", [P, NT, 2, KD, P])
        shi = s.sb("shi", [P, 2, KD, R], F32R)
        slo = s.sb("slo", [P, 2, KD, R], F32R)
        nhi = s.sb("nhi", [P, KD, R], F32R)
        nlo = s.sb("nlo", [P, KD, R], F32R)
        sqm = s.sb("sqm", [P, 2, R])
        amp = s.sb("amp", [P, KD, R])
        ahi = s.sb("ahi", [P, KD, R], F32R)
        alo = s.sb("alo", [P, KD, R], F32R)
        u = s.sb("u", [P, NT, W])
        ust = s.sb("ust", [P, NT, 6])
        umv = s.sb("umv", [P, NT, 2])
        usd = s.sb("usd", [P, NT])
        uri = s.sb("uri", [P, NT])
        z = s.sb("z", [P, KD, R])
        zhi = s.sb("zhi", [P, KD, R], F32R)
        zlo = s.sb("zlo", [P, KD, R], F32R)
        tx = s.sb("tx", [P, NT, W])
        r = s.sb("r", [P, KD, R])
        rhi = s.sb("rhi", [P, KD, R], F32R)
        rlo = s.sb("rlo", [P, KD, R], F32R)
        yt = s.sb("yt", [P, NT, TOP2])
        yj = s.sb("yj", [P, NT, TOP2])
        y2 = s.sb("y2", [P, NT])
        y = s.sb("y", [P, TT])
        w_loaded = [s.sem(f"w_loaded{i}") for i in range(TR)]
        row_in, w_hi, w_split = s.sem("row_in"), s.sem("w_hi"), s.sem("w_split")
        sup_in, tx_in = s.sem("sup_in"), s.sem("tx_in")
        s_turned = s.sem("s_turned")
        s_hi, s_split = s.sem("s_hi"), s.sem("s_split")
        negated = s.sem("negated")
        measured = s.sem("measured")
        m_squared = s.sem("m_squared")
        m_summed = s.sem("m_summed")
        amp_done = s.sem("amp_done")
        a_hi, a_split = s.sem("a_hi"), s.sem("a_split")
        posted = s.sem("posted")
        u_read = s.sem("u_read")
        u_step = s.sem("u_step")
        sd_done = s.sem("sd_done")
        u_ready = s.sem("u_ready")
        z_turned = s.sem("z_turned")
        z_done = s.sem("z_done")
        z_hi, z_split = s.sem("z_hi"), s.sem("z_split")
        top1 = s.sem("top1")
        t1_read = s.sem("t1_read")
        r_turned = s.sem("r_turned")
        r_done = s.sem("r_done")
        r_hi, r_split = s.sem("r_hi"), s.sem("r_split")
        top2 = s.sem("top2")
        y_step = s.sem("y_step")
        y_done = s.sem("y_done")
        out_done = s.sem("out_done")
        block = s.ctx.enter_context(nc.Block())

        def pipeline(eng, body):
            body(0, None)
            body(1, 0)
            with eng.Fori(2, NB) as t:
                body(t, t - 1)
            body(None, NB - 1)

        def flat(t):
            return t.rearrange("p k n -> p (k n)")

        @block.sync
        def _(sp):
            def body(t):
                sp.wait_ge(s_turned, t * 4)
                sp.dma_start(sup[:, :, :, :, :].rearrange("p t a k n -> p t (a k n)"),
                             g.sup_scr[bass.ds(t * NT, NT)].rearrange("t p a n -> p t (a n)")).then_inc(sup_in, 16)
                sp.wait_ge(r_turned, t * 2)
                sp.dma_start(tx[:, :, :], g.h_scr[CHUNKS_A - 1, bass.ds(t * NT, NT)].rearrange(
                    "t p n -> p t n")).then_inc(tx_in, 16)

            body(0)
            for i in range(NP):
                if i >= TR:
                    sp.wait_ge(w_split, i - TR + 1)
                sp.dma_start(wraw[:, i % TR, :], g.w_pieces[PC_TOP + i]).then_inc(w_loaded[i % TR], 16)
            sp.dma_start(row[:, :], g.row2.rearrange("o n -> (o n)").partition_broadcast(P)).then_inc(row_in, 16)
            with sp.Fori(1, NB) as t:
                body(t)
            sp.wait_ge(y_done, NB)
            sp.dma_start(g.out.rearrange("(t p) o -> p (t o)", p=P), y[:, :], allow_slow_non_contiguous=True).then_inc(out_done, 16)
            sp.wait_ge(out_done, 16)

        @block.gpsimd
        def _(pool):
            def negate(t):
                pool.wait_ge(s_split, t * 4 + 4)
                pool.wait_ge(measured, t * 4)
                for n, x in ((nhi, shi), (nlo, slo)):
                    pool.tensor_tensor(flat(n), g.none[:, :].to_broadcast([P, KD * R]), flat(x[:, 1].bitcast(F32)),
                                       ALU.subtract).then_inc(negated, 1)

            negate(0)
            with pool.Fori(1, NB) as t:
                negate(t)

        @block.scalar
        def _(act):
            def sup_high(t):
                for q in range(4):
                    act.wait_ge(s_turned, t * 4 + (q + 1))
                    act.wait_ge(measured, t * 4)
                    act.activation(shi[:, q // 2, 2 * (q % 2):2 * (q % 2) + 2, :].rearrange("p k n -> p (k n)"),
                                   g.ps[:, q % 2, :], ACT.Copy).then_inc(s_hi, 1)

            def amplitude(t, m):
                act.wait_ge(measured, t * 4 + (m + 1))
                act.wait_ge(m_summed, t * 4 + m)
                act.activation(sqm[:, :, :].rearrange("p a n -> p (a n)"), g.ps[:, 2 + m % 2, :],
                               ACT.Square).then_inc(m_squared, 1)
                act.wait_ge(m_summed, t * 4 + (m + 1))
                act.activation(amp[:, m, :], amp[:, m, :], ACT.Sqrt).then_inc(amp_done, 1)
                act.wait_ge(amp_done, t * 4 + (m + 1))
                act.wait_ge(posted, t * 2)
                act.activation(ahi[:, m, :], amp[:, m, :], ACT.Copy).then_inc(a_hi, 1)

            def deviation(t):
                act.wait_ge(u_step, t * 4 + 3)
                act.activation(usd[:, :], umv[:, :, 1], ACT.Sqrt, bias=g.eps_ln[:, :]).then_inc(sd_done, 1)

            def gelu(t):
                for k in range(KD):
                    act.wait_ge(z_turned, t * 2 + (k // 2 + 1))
                    act.wait_ge(z_split, t)
                    act.activation(z[:, k, :], g.ps[:, 6 + k // 2, (k % 2) * R:(k % 2 + 1) * R], ACT.Gelu,
                                   bias=g.cols[:, COL_PBE + k:COL_PBE + k + 1],
                                   scale=g.cols[:, COL_PG + k:COL_PG + k + 1]).then_inc(z_done, 1)
                act.wait_ge(z_done, t * 4 + 4)
                act.wait_ge(top1, t * 2)
                act.activation(flat(zhi), flat(z), ACT.Copy).then_inc(z_hi, 1)

            def relu(t):
                for q in range(2):
                    act.wait_ge(r_turned, t * 2 + (q + 1))
                    act.wait_ge(r_split, t)
                    act.activation(r[:, 2 * q:2 * q + 2, :].rearrange("p k n -> p (k n)"), g.ps[:, 6 + q, :],
                                   ACT.Relu).then_inc(r_done, 1)
                act.wait_ge(r_done, t * 2 + 2)
                act.wait_ge(top2, t)
                act.activation(flat(rhi), flat(r), ACT.Copy).then_inc(r_hi, 1)

            def pieces(i0, i1):
                for i in range(i0, i1):
                    act.wait_ge(w_loaded[i % TR], 16 * (i // TR + 1))
                    act.activation(whi[:, i, :], wraw[:, i % TR, :], ACT.Copy).then_inc(w_hi, 1)

            def body(t1, t2):
                if t1 is not None:
                    sup_high(t1)
                if t2 is None:
                    pieces(0, NP)
                if t2 is not None:
                    deviation(t2)
                if t1 is not None:
                    amplitude(t1, 0)
                    amplitude(t1, 1)
                if t2 is not None:
                    gelu(t2)
                if t1 is not None:
                    amplitude(t1, 2)
                    amplitude(t1, 3)
                if t2 is not None:
                    relu(t2)

            pipeline(act, body)

        @block.vector
        def _(dve):
            def sup_low(t):
                for q in range(4):
                    dve.wait_ge(s_hi, t * 4 + (q + 1))
                    if q == 0:
                        dve.wait_ge(negated, t * 2)
                    dve.tensor_tensor(slo[:, q // 2, 2 * (q % 2):2 * (q % 2) + 2, :].rearrange("p k n -> p (k n)"),
                                      g.ps[:, q % 2, :], shi[:, q // 2, 2 * (q % 2):2 * (q % 2) + 2, :].bitcast(F32).rearrange(
                                          "p k n -> p (k n)"), ALU.subtract).then_inc(s_split, 1)

            def amplitude(t, m):
                dve.wait_ge(m_squared, t * 4 + (m + 1))
                dve.tensor_tensor(amp[:, m, :], sqm[:, 0, :], sqm[:, 1, :], ALU.add).then_inc(m_summed, 1)
                dve.wait_ge(a_hi, t * 4 + (m + 1))
                dve.tensor_tensor(alo[:, m, :], amp[:, m, :], ahi[:, m, :].bitcast(F32), ALU.subtract).then_inc(a_split, 1)

            def post(t):
                for i in range(NT):
                    dve.wait_ge(posted, t * 2 + (i + 1))
                    if i == 0:
                        dve.wait_ge(z_turned, t * 2)
                    dve.tensor_tensor(u[:, i, :], g.ps[:, 4 + i, :], row[:, 0:W], ALU.add).then_inc(u_read, 1)
                dve.wait_ge(u_read, t * 2 + 2)
                for i in range(NT):
                    ins = dve.bn_stats(ust[:, i, :], u[:, i, :])
                ins.then_inc(u_step, 1)
                dve.wait_ge(u_step, t * 4 + 1)
                dve.tensor_scalar(uri[:, :], ust[:, :, 1], 0.0, None, ALU.mult)
                for i in range(NT):
                    dve.bn_aggr(umv[:, i, :], ust[:, i, :]).then_inc(u_step, 1)
                dve.wait_ge(sd_done, t + 1)
                dve.reciprocal(uri[:, :], usd[:, :]).then_inc(u_step, 1)
                dve.wait_ge(u_step, t * 4 + 4)
                for i in range(NT):
                    ins = dve.tensor_scalar(u[:, i, :], u[:, i, :], umv[:, i, 0:1], uri[:, i:i + 1], ALU.subtract, ALU.mult)
                ins.then_inc(u_ready, 1)

            def z_low(t):
                dve.wait_ge(z_hi, t + 1)
                dve.tensor_tensor(flat(zlo), flat(z), flat(zhi).bitcast(F32), ALU.subtract).then_inc(z_split, 1)

            def add_rx(t):
                dve.wait_ge(tx_in, t * 16 + 16)
                for i in range(NT):
                    dve.wait_ge(top1, t * 2 + (i + 1))
                    dve.tensor_tensor(tx[:, i, :], g.ps[:, 4 + i, :], tx[:, i, :], ALU.add).then_inc(t1_read, 1)

            def r_low(t):
                dve.wait_ge(r_hi, t + 1)
                dve.tensor_tensor(flat(rlo), flat(r), flat(rhi).bitcast(F32), ALU.subtract).then_inc(r_split, 1)

            def output(t):
                dve.wait_ge(top2, t + 1)
                dve.tensor_tensor(yt[:, :, :], g.ps[:, 4, :].rearrange("p (t n) -> p t n", t=NT),
                                  row[:, W:W + TOP2].unsqueeze(1).to_broadcast([P, NT, TOP2]), ALU.add).then_inc(y_step, 1)
                dve.wait_ge(y_step, t * 3 + 1)
                for i in range(NT):
                    dve.scalar_tensor_tensor(out=yj[:, i, :], in0=yt[:, i, :], scalar=0.0, in1=row[:, W + TOP2:2 * W],
                                             op0=ALU.max, op1=ALU.mult, accum_out=y2[:, i:i + 1]).then_inc(y_step, 1)
                dve.wait_ge(y_step, t * 3 + 3)
                dve.tensor_copy(y[:, bass.ds(t * NT, NT)], y2[:, :]).then_inc(y_done, 1)

            def pieces(i0, i1):
                for i in range(i0, i1):
                    dve.wait_ge(w_hi, i + 1)
                    dve.tensor_tensor(wlo[:, i, :], wraw[:, i % TR, :], whi[:, i, :].bitcast(F32),
                                      ALU.subtract).then_inc(w_split, 1)

            def body(t1, t2):
                if t1 is not None:
                    sup_low(t1)
                if t2 is None:
                    pieces(0, NP)
                    dve.wait_ge(row_in, 16)
                if t2 is not None:
                    post(t2)
                if t1 is not None:
                    amplitude(t1, 0)
                    amplitude(t1, 1)
                if t2 is not None:
                    z_low(t2)
                if t1 is not None:
                    amplitude(t1, 2)
                if t2 is not None:
                    add_rx(t2)
                if t1 is not None:
                    amplitude(t1, 3)
                if t2 is not None:
                    r_low(t2)
                    output(t2)

            pipeline(dve, body)

        @block.tensor
        def _(pe):
            def turn_sup(t):
                pe.wait_ge(sup_in, t * 16 + 16)
                for q in range(4):
                    pe.wait_ge(s_split, t * 4 + 2 * (q // 2))
                    for k in (2 * (q % 2), 2 * (q % 2) + 1):
                        for i in range(NT):
                            mm = pe.transpose(g.ps[:, q % 2, (k % 2) * R + i * P:(k % 2) * R + (i + 1) * P],
                                              sup[:, i, q // 2, k, :], g.ident[:, :])
                    mm.then_inc(s_turned, 1)

            def measure(t, m):
                pe.wait_ge(w_split, W_POST)
                pe.wait_ge(s_split, t * 4 + 4)
                pe.wait_ge(negated, t * 2 + 2)
                if not isinstance(t, int) or 4 * t + m >= 2:
                    pe.wait_ge(m_squared, t * 4 + (m - 1))
                mc = slice(m * P, (m + 1) * P)
                for part in range(2):
                    terms = (((W_MR, shi[:, 0], slo[:, 0]), (W_MI, nhi, nlo)) if part == 0 else
                             ((W_MI, shi[:, 0], slo[:, 0]), (W_MR, shi[:, 1], slo[:, 1])))
                    for x, (w, hi, lo) in enumerate(terms):
                        for k in range(KD):
                            mm = split3(pe.matmul, g.ps[:, 2 + m % 2, part * R:(part + 1) * R], whi[:, w + k, mc],
                                        wlo[:, w + k, mc], hi[:, k, :], lo[:, k, :], x == 0 and k == 0,
                                        x == 1 and k == KD - 1)
                mm.then_inc(measured, 1)

            def rows_layer(bank, cols, hi, lo, piece, i, width=W, offset=0):
                for k in range(KD):
                    if width == W:
                        wh, wl = whi[:, piece + k, :], wlo[:, piece + k, :]
                    else:
                        c = slice((k % 2) * width, (k % 2 + 1) * width)
                        wh, wl = whi[:, piece + k // 2, c], wlo[:, piece + k // 2, c]
                    mm = split3(pe.matmul, g.ps[:, bank, cols], hi[:, k, i * P:(i + 1) * P], lo[:, k, i * P:(i + 1) * P],
                                wh, wl, k == 0, k == KD - 1)
                return mm

            def post(t):
                pe.wait_ge(w_split, W_T1)
                pe.wait_ge(a_split, t * 4 + 4)
                pe.wait_ge(t1_read, t * 2)
                pe.wait_ge(y_step, t * 3)
                for i in range(NT):
                    rows_layer(4 + i, slice(0, W), ahi, alo, W_POST, i).then_inc(posted, 1)

            def turn(src, bank, done):
                for q in range(2):
                    for k in (2 * q, 2 * q + 1):
                        for i in range(NT):
                            mm = pe.transpose(g.ps[:, bank + q, (k % 2) * R + i * P:(k % 2) * R + (i + 1) * P],
                                              src[:, i, k * P:(k + 1) * P], g.ident[:, :])
                    mm.then_inc(done, 1)

            def turn_z(t):
                pe.wait_ge(u_ready, t + 1)
                pe.wait_ge(r_done, t * 2)
                turn(u, 6, z_turned)

            def top_one(t):
                pe.wait_ge(w_split, W_T2)
                pe.wait_ge(z_split, t + 1)
                pe.wait_ge(u_read, t * 2 + 2)
                for i in range(NT):
                    rows_layer(4 + i, slice(0, W), zhi, zlo, W_T1, i).then_inc(top1, 1)

            def turn_r(t):
                pe.wait_ge(t1_read, t * 2 + 2)
                pe.wait_ge(z_done, t * 4 + 4)
                turn(tx, 6, r_turned)

            def top_two(t):
                pe.wait_ge(w_split, NP)
                pe.wait_ge(r_split, t + 1)
                for i in range(NT):
                    mm = rows_layer(4, slice(i * TOP2, (i + 1) * TOP2), rhi, rlo, W_T2, i, TOP2)
                mm.then_inc(top2, 1)

            def body(t1, t2):
                if t1 is not None:
                    turn_sup(t1)
                if t2 is not None:
                    post(t2)
                if t1 is not None:
                    measure(t1, 0)
                    measure(t1, 1)
                if t2 is not None:
                    turn_z(t2)
                if t1 is not None:
                    measure(t1, 2)
                if t2 is not None:
                    top_one(t2)
                if t1 is not None:
                    measure(t1, 3)
                if t2 is not None:
                    turn_r(t2)
                    top_two(t2)

            pipeline(pe, body)


def build(nc, g):
    with ExitStack() as ctx:
        g.ps = ctx.enter_context(nc.psum_tensor("banks", [P, 8, W], F32))
        g.cols = ctx.enter_context(nc.sbuf_tensor("cols", [P, NCOL], F32))
        g.ident = ctx.enter_context(nc.sbuf_tensor("ident", [P, P], F32))
        g.mask = ctx.enter_context(nc.sbuf_tensor("mask", [P, N, GB], F32))
        g.eps_ln = ctx.enter_context(nc.sbuf_tensor("eps_ln", [P, 1], F32))
        g.tiny = ctx.enter_context(nc.sbuf_tensor("tiny", [P, 1], F32))
        g.none = ctx.enter_context(nc.sbuf_tensor("none", [P, 1], F32))
        g.tiny_hd = ctx.enter_context(nc.sbuf_tensor("tiny_hd", [P, 1], F32))
        phase_constants(nc, g)
        with nc.sbuf_tensor("stats", [P, CHUNKS_A * TT, 6], F32) as g.stats:
            phase_first_layers(nc, g)
            phase_second_layers(nc, g)
        phase_attention(nc, g)
        phase_interfere(nc, g)
        phase_top(nc, g)


class Tensors:
    pass


def layout(inputs):
    import numpy as np
    a = {k: np.asarray(v) for k, v in inputs.items()}
    e = lambda n: a["L0_rec_" + n]
    out = {}
    out["x_t"] = a["r_x"].T.reshape(KI, P, TOK)
    first = [e(b + "_W1").T.reshape(KI, P, 4, W)[:, :, c] for b in ("er", "ei") for c in range(4)]
    first.append(a["W_top1"][OUT:].reshape(KI, P, W))
    out["w_first"] = np.stack(first)
    out["row1"] = np.concatenate([e("er_b1").reshape(4, W), e("ei_b1").reshape(4, W), a["b_top1"].reshape(1, W)])
    second = [e(b + "_W2").T.reshape(8, 2, P, 2, 2, KD, P).transpose(5, 3, 0, 2, 1, 4, 6).reshape(8, 8, P, W)
              for b in ("er", "ei")]
    out["w_second"] = np.concatenate(second)

    def cols(v):
        return v.reshape(-1, P).T
    by_chunk = {n: e(n).reshape(N, KD, P).transpose(1, 0, 2) for n in ("er_b2", "ei_b2")}
    out["cols_in"] = np.concatenate([cols(by_chunk.get(n, e(n)) if n in by_chunk else e(n)) for n in (
        "er_g1", "er_be1", "ei_g1", "ei_be1", "er_b2", "ei_b2", "bq_r", "bq_i", "bk_r", "bk_i", "bv_r", "bv_i",
        "bo_r", "bo_i", "post_g", "post_be")] + [
            np.stack([e("bv_r").reshape(H, HD), e("bv_i").reshape(H, HD)]).transpose(0, 2, 1).reshape(P, H)], axis=1)
    pieces = []
    for n in ("Wq_r", "Wq_i", "Wk_r", "Wk_i", "Wv_r", "Wv_i", "Wo_r", "Wo_i"):
        pieces.append(e(n).T.reshape(KD, P, W))
    for n in range(N):
        for t in ("int_Wr", "int_Wi"):
            pieces.append(e(t)[n].T.reshape(KD, P, W))
    for n in ("meas_Mr", "meas_Mi", "post_W"):
        pieces.append(e(n).T.reshape(KD, P, W))
    pieces.append(a["W_top1"][:OUT].reshape(KD, P, W))
    pieces.append(a["W_top2"].reshape(2, 2, P, TOP2).transpose(0, 2, 1, 3).reshape(2, P, W))
    out["w_pieces"] = np.concatenate(pieces)
    out["row2"] = np.concatenate([e("post_b"), a["b_top2"], a["W_top3"][:, 0]]).reshape(1, 1024)
    out["ids"] = a["ids"]
    for f in range(N):
        out[f"tbl_{f}"] = a[f"tbl_{f}"]
    return {k: np.ascontiguousarray(v) for k, v in out.items()}


def program(nc, arrays):
    def tensor(name):
        v = arrays[name]
        return nc.dram_tensor(name, v.shape, mybir.dt.from_np(v.dtype), kind="ExternalInput").ap()

    g = Tensors()
    g.x_t, g.w_first, g.row1 = tensor("x_t"), tensor("w_first"), tensor("row1")
    g.w_second, g.cols_in = tensor("w_second"), tensor("cols_in")
    g.w_pieces, g.row2, g.ids = tensor("w_pieces"), tensor("row2"), tensor("ids")
    g.tbl_0, g.tbl_1, g.tbl_2, g.tbl_3 = tensor("tbl_0"), tensor("tbl_1"), tensor("tbl_2"), tensor("tbl_3")
    g.out = nc.dram_tensor("out", (TOK, 1), F32, kind="ExternalOutput").ap()
    g.h_scr = nc.dram_tensor("h_scr", (CHUNKS_A, TT, P, W), F32, kind="Internal").ap()
    g.s_scr = nc.dram_tensor("s_scr", (2, 2, TOK // GB, P, KD, N, GB), F32, kind="Internal").ap()
    g.a_scr = nc.dram_tensor("a_scr", (TOK // BT, N, P, 4, KD, BT), F32, kind="Internal").ap()
    g.sup_scr = nc.dram_tensor("sup_scr", (TT, P, 2, D), F32, kind="Internal").ap()
    build(nc, g)
    return g


def kernel(**inputs):
    import concourse.bacc as bacc
    from concourse.bass_utils import run_bass_kernel_spmd

    arrays = layout(inputs)
    nc = bacc.Bacc("TRN2", target_bir_lowering=False, num_devices=1)
    program(nc, arrays)
    r = run_bass_kernel_spmd(nc, [arrays], core_ids=[0])
    return r.results[0]["out"]
```
